# Optimizing a Trainium2 kernel written in Bass

```python
import numpy as np
import jax
import jax.numpy as jnp

def _softmax(x, axis=-1):
    return jax.nn.softmax(x, axis=axis)

def _gelu(x):
    return jax.nn.gelu(x, approximate=True)

def _silu(x):
    return jax.nn.silu(x)

def _sigmoid(x):
    return jax.nn.sigmoid(x)

def _layernorm(x, axis=-1, eps=1e-05):
    m = jnp.mean(x, axis=axis, keepdims=True)
    v = jnp.var(x, axis=axis, keepdims=True)
    return (x - m) / jnp.sqrt(v + eps)

def _scatter_add(tgt, idx, src, axis=0):
    return tgt.at[idx].add(src)

def _segment_sum(src, seg, n):
    return jax.ops.segment_sum(src, seg, n)
kernel_name = 'mk_vit_tower_d4_tok_img768_r4_85742b'

def setup_inputs(seed: int=0):
    np.random.seed(seed)
    _w = jnp.asarray

    def _rec_inputs():
        import jax
        import jax.numpy as jnp
        _rk = jax.random.key(seed)
        x = -0.00040386 + 0.999972 * jax.random.normal(jax.random.fold_in(_rk, 1), (64, 64, 64, 3), jnp.float32)
        return x
    x = _rec_inputs()

    def _L0_tok_setup():
        import jax, jax.numpy as jnp
        import numpy as np
        PATCH = 16
        key = jax.random.key(seed)
        k1, k2, k3 = jax.random.split(key, 3)
        B, H, Wd, C = (64, 64, 64, 3)
        patch_dim = PATCH * PATCH * C
        hidden = 192
        num_patches = H // PATCH * (Wd // PATCH)
        img = jax.random.normal(k1, (B, H, Wd, C), dtype=jnp.float32)
        W = jax.random.normal(k2, (patch_dim, hidden), dtype=jnp.float32) * (1.0 / np.sqrt(patch_dim))
        b = jnp.zeros((hidden,), dtype=jnp.float32)
        pos_emb = jax.random.normal(k3, (num_patches, hidden), dtype=jnp.float32) * 0.02
        return {'img': img, 'W': W, 'b': b, 'pos_emb': pos_emb}
    _L0_tok_all = _L0_tok_setup()
    _L0_tok_in = {k: v for k, v in _L0_tok_all.items() if k in ('W', 'b', 'pos_emb')}
    del _L0_tok_all

    def _L0_attn_setup():
        import jax, jax.numpy as jnp
        import numpy as np
        B, S, E, H = (8, 512, 192, 1)
        HD = E // H
        LR = 0.01

        def _apply_delays(spikes, delay_weights):
            b, s, e = spikes.shape
            t = jnp.arange(s)
            src = t[:, None, None] - delay_weights[None, :, :]
            valid = src >= 0
            src_c = jnp.clip(src, 0, s - 1)
            g = spikes[:, src_c, jnp.arange(e)[None, None, :]]
            return jnp.sum(jnp.where(valid[None], g, jnp.float32(0)), axis=2)
        key = jax.random.key(seed)
        ks = jax.random.split(key, 7)
        spikes = jax.random.normal(ks[0], (B, S, E), dtype=jnp.float32)
        delay_weights = jax.random.randint(ks[1], (H, E), 1, 16, dtype=jnp.int32)
        membrane_potentials = jnp.zeros((H, E), dtype=jnp.float32)
        decay_constant = jnp.float32(0.9)
        scale = 0.02
        Wq = jax.random.normal(ks[2], (E, E), dtype=jnp.float32) * scale
        Wk = jax.random.normal(ks[3], (E, E), dtype=jnp.float32) * scale
        Wv = jax.random.normal(ks[4], (E, E), dtype=jnp.float32) * scale
        Wo = jax.random.normal(ks[5], (E, E), dtype=jnp.float32) * scale
        bo = jnp.zeros((E,), dtype=jnp.float32)
        return {'spikes': spikes, 'delay_weights': delay_weights, 'membrane_potentials': membrane_potentials, 'decay_constant': decay_constant, 'Wq': Wq, 'Wk': Wk, 'Wv': Wv, 'Wo': Wo, 'bo': bo}
    _L0_attn_all = _L0_attn_setup()
    _L0_attn_in = {k: v for k, v in _L0_attn_all.items() if k in ('delay_weights', 'membrane_potentials', 'decay_constant', 'Wq', 'Wk', 'Wv', 'Wo', 'bo')}
    del _L0_attn_all

    def _L0_ffn_setup():
        import jax, jax.numpy as jnp
        import numpy as np
        B, S, H = (4, 2048, 192)
        E, K = (8, 2)
        key = jax.random.key(seed)
        ks = jax.random.split(key, 5)
        scale = 1.0 / np.sqrt(H)
        x = jax.random.normal(ks[0], (B, S, H), dtype=jnp.float32)
        router_w = jax.random.uniform(ks[1], (E, H), jnp.float32, -scale, scale)
        router_b = jax.random.uniform(ks[2], (E,), jnp.float32, -scale, scale)
        expert_w = jax.random.uniform(ks[3], (E, H, H), jnp.float32, -scale, scale)
        expert_b = jax.random.uniform(ks[4], (E, H), jnp.float32, -scale, scale)
        return {'x': x, 'router_w': router_w, 'router_b': router_b, 'expert_w': expert_w, 'expert_b': expert_b}
    _L0_ffn_all = _L0_ffn_setup()
    _L0_ffn_in = {k: v for k, v in _L0_ffn_all.items() if k in ('router_w', 'router_b', 'expert_w', 'expert_b')}
    del _L0_ffn_all

    def _L1_attn_setup():
        import jax, jax.numpy as jnp
        import numpy as np
        LEVEL = 8
        NUM_HEADS = 12
        QN_SYM = float(-(LEVEL // 2))
        QP_SYM = float(LEVEL // 2 - 1)
        QN_ASYM = 0.0
        QP_ASYM = float(LEVEL - 1)

        def fake_quant(x, s, qn, qp):
            xc = jnp.clip(x / s, qn, qp)
            xr = xc + jax.lax.stop_gradient(jnp.round(xc) - xc)
            return s * xr
        key = jax.random.key(seed)
        k0, k1, k2 = jax.random.split(key, 3)
        B, N, C = (4, 512, 192)
        x = jax.random.normal(k0, (B, N, C), dtype=jnp.float32)
        Wqkv = jax.random.normal(k1, (3 * C, C), dtype=jnp.float32) * C ** (-0.5)
        Wproj = jax.random.normal(k2, (C, C), dtype=jnp.float32) * C ** (-0.5)
        bproj = jnp.zeros((C,), dtype=jnp.float32)
        s_q = jnp.asarray(1.0, dtype=jnp.float32)
        s_k = jnp.asarray(1.0, dtype=jnp.float32)
        s_v = jnp.asarray(1.0, dtype=jnp.float32)
        s_attn = jnp.asarray(1.0 / QP_ASYM, dtype=jnp.float32)
        s_after = jnp.asarray(1.0, dtype=jnp.float32)
        return {'x': x, 'Wqkv': Wqkv, 'Wproj': Wproj, 'bproj': bproj, 's_q': s_q, 's_k': s_k, 's_v': s_v, 's_attn': s_attn, 's_after': s_after}
    _L1_attn_all = _L1_attn_setup()
    _L1_attn_in = {k: v for k, v in _L1_attn_all.items() if k in ('Wqkv', 'Wproj', 'bproj', 's_q', 's_k', 's_v', 's_attn', 's_after')}
    del _L1_attn_all

    def _L1_ffn_setup():
        import jax, jax.numpy as jnp
        import numpy as np
        B, S, D, F = (2, 128, 192, 768)
        L, H, DK = (4, 12, 64)
        E, K = (8, 2)
        NB, MAXD = (32, 128)
        MOE_LAYERS = (1, 3)
        EPS = 1e-06

        def t5_layer_norm(x, w):
            var = jnp.mean(x * x, axis=-1, keepdims=True)
            return w * x * jax.lax.rsqrt(var + EPS)

        def relative_position_bias(rel_emb, seq_len):
            ctx = jnp.arange(seq_len)[:, None]
            mem = jnp.arange(seq_len)[None, :]
            rel = mem - ctx
            nb = NB // 2
            buckets = (rel > 0).astype(jnp.int32) * nb
            n = jnp.abs(rel)
            max_exact = nb // 2
            is_small = n < max_exact
            nf = jnp.maximum(n, 1).astype(jnp.float32)
            large = max_exact + (jnp.log(nf / max_exact) / np.log(MAXD / max_exact) * (nb - max_exact)).astype(jnp.int32)
            large = jnp.minimum(large, nb - 1)
            buckets = buckets + jnp.where(is_small, n, large)
            return rel_emb[buckets].transpose(2, 0, 1)[None]

        def moe_ffn(x2d, gw, w1, w2):
            logits = x2d @ gw
            vals, idx = jax.lax.top_k(logits, K)
            gsc = jax.nn.softmax(vals, axis=-1)
            T = x2d.shape[0]
            cw = jnp.zeros((T, E), x2d.dtype).at[jnp.arange(T)[:, None], idx].add(gsc)

            def body(acc, xs):
                w1e, w2e, cwe = xs
                y = jax.nn.gelu(x2d @ w1e, approximate=False) @ w2e
                return (acc + cwe[:, None] * y, None)
            out, _ = jax.lax.scan(body, jnp.zeros_like(x2d), (w1, w2, cw.T))
            return out
        key = jax.random.key(seed)
        ks = list(jax.random.split(key, 16))

        def nrm(k, shape, scale=0.02):
            return jax.random.normal(k, shape, jnp.float32) * scale
        M = len(MOE_LAYERS)
        return {'x': nrm(ks[0], (B, S, D), 1.0), 'attn_q': nrm(ks[1], (L, D, H * DK)), 'attn_k': nrm(ks[2], (L, D, H * DK)), 'attn_v': nrm(ks[3], (L, D, H * DK)), 'attn_o': nrm(ks[4], (L, H * DK, D)), 'ffn_wi': nrm(ks[5], (L, D, F)), 'ffn_wo': nrm(ks[6], (L, F, D)), 'ln1': jnp.ones((L, D), jnp.float32), 'ln2': jnp.ones((L, D), jnp.float32), 'ln_f': jnp.ones((D,), jnp.float32), 'rel_emb': nrm(ks[7], (NB, H), 0.1), 'gate_w': nrm(ks[8], (M, D, E)), 'moe_w1': nrm(ks[9], (M, E, D, F)), 'moe_w2': nrm(ks[10], (M, E, F, D))}
    _L1_ffn_all = _L1_ffn_setup()
    _L1_ffn_in = {k: v for k, v in _L1_ffn_all.items() if k in ('attn_q', 'attn_k', 'attn_v', 'attn_o', 'ffn_wi', 'ffn_wo', 'ln1', 'ln2', 'ln_f', 'rel_emb', 'gate_w', 'moe_w1', 'moe_w2')}
    del _L1_ffn_all

    def _L2_attn_setup():
        import jax, jax.numpy as jnp
        import numpy as np
        B, L, D, H = (2, 512, 192, 12)
        HD = D // H
        ROPE_BASE = 10000.0

        def apply_rope(x):
            d = x.shape[-1]
            pos = jnp.arange(x.shape[2], dtype=jnp.float32)
            inv_freq = 1.0 / ROPE_BASE ** (jnp.arange(0, d, 2, dtype=jnp.float32) / d)
            ang = pos[:, None] * inv_freq[None, :]
            cos = jnp.concatenate([jnp.cos(ang), jnp.cos(ang)], axis=-1)
            sin = jnp.concatenate([jnp.sin(ang), jnp.sin(ang)], axis=-1)
            x1, x2 = jnp.split(x, 2, axis=-1)
            rot = jnp.concatenate([-x2, x1], axis=-1)
            return x * cos[None, None, :, :].astype(x.dtype) + rot * sin[None, None, :, :].astype(x.dtype)
        key = jax.random.key(seed)
        ks = jax.random.split(key, 9)
        s = 1.0 / np.sqrt(D)
        return {'query': jax.random.normal(ks[0], (B, L, D), dtype=jnp.float32), 'Wq': jax.random.uniform(ks[1], (D, D), jnp.float32, -s, s), 'bq': jax.random.uniform(ks[2], (D,), jnp.float32, -s, s), 'Wk': jax.random.uniform(ks[3], (D, D), jnp.float32, -s, s), 'bk': jax.random.uniform(ks[4], (D,), jnp.float32, -s, s), 'Wv': jax.random.uniform(ks[5], (D, D), jnp.float32, -s, s), 'bv': jax.random.uniform(ks[6], (D,), jnp.float32, -s, s), 'Wo': jax.random.uniform(ks[7], (D, D), jnp.float32, -s, s), 'bo': jax.random.uniform(ks[8], (D,), jnp.float32, -s, s)}
    _L2_attn_all = _L2_attn_setup()
    _L2_attn_in = {k: v for k, v in _L2_attn_all.items() if k in ('Wq', 'bq', 'Wk', 'bk', 'Wv', 'bv', 'Wo', 'bo')}
    del _L2_attn_all

    def _L2_ffn_setup():
        import jax, jax.numpy as jnp
        import numpy as np
        D_MODEL = 192
        N_EXPERTS = 16
        TOP_K = 2
        D_FF = 4 * D_MODEL
        B, L = (4, 512)
        key = jax.random.key(seed)
        ks = jax.random.split(key, 6)
        s_in = 1.0 / np.sqrt(D_MODEL)
        s_ff = 1.0 / np.sqrt(D_FF)
        x = jax.random.normal(ks[0], (B, L, D_MODEL), dtype=jnp.float32)
        Wr = jax.random.uniform(ks[1], (N_EXPERTS, D_MODEL), jnp.float32, -s_in, s_in)
        W1 = jax.random.uniform(ks[2], (N_EXPERTS, D_MODEL, D_FF), jnp.float32, -s_in, s_in)
        b1 = jax.random.uniform(ks[3], (N_EXPERTS, D_FF), jnp.float32, -s_in, s_in)
        W2 = jax.random.uniform(ks[4], (N_EXPERTS, D_FF, D_MODEL), jnp.float32, -s_ff, s_ff)
        b2 = jax.random.uniform(ks[5], (N_EXPERTS, D_MODEL), jnp.float32, -s_ff, s_ff)
        return {'x': x, 'Wr': Wr, 'W1': W1, 'b1': b1, 'W2': W2, 'b2': b2}
    _L2_ffn_all = _L2_ffn_setup()
    _L2_ffn_in = {k: v for k, v in _L2_ffn_all.items() if k in ('Wr', 'W1', 'b1', 'W2', 'b2')}
    del _L2_ffn_all

    def _L3_attn_setup():
        import jax, jax.numpy as jnp
        import numpy as np
        EMBED_DIM = 192
        NUM_HEADS = 12
        HEAD_DIM = EMBED_DIM // NUM_HEADS
        MAX_WAVELENGTH = 10000.0
        ROPE_PERCENT = 0.5

        def p_rope(x, positions):
            rope_angles = int(ROPE_PERCENT * HEAD_DIM) // 2
            nope_angles = HEAD_DIM // 2 - rope_angles
            fraction = 2.0 * jnp.arange(rope_angles, dtype=x.dtype) / HEAD_DIM
            timescale = MAX_WAVELENGTH ** fraction
            timescale = jnp.concatenate([timescale, jnp.full((nope_angles,), jnp.inf, dtype=x.dtype)])
            sinusoid = positions[:, None] / timescale[None, :]
            sin, cos = (jnp.sin(sinusoid), jnp.cos(sinusoid))
            x1, x2 = jnp.split(x, 2, axis=-1)
            return jnp.concatenate([x1 * cos - x2 * sin, x2 * cos + x1 * sin], axis=-1)

        def _shape(x, B, S):
            return x.reshape(B, S, NUM_HEADS, HEAD_DIM).transpose(0, 2, 1, 3).reshape(B * NUM_HEADS, S, HEAD_DIM)
        key = jax.random.key(seed)
        ks = jax.random.split(key, 9)
        B, T, E = (16, 256, EMBED_DIM)
        s = 0.02
        return {'hidden_states': jax.random.normal(ks[0], (B, T, E), jnp.float32), 'wq': jax.random.normal(ks[1], (E, E), jnp.float32) * s, 'bq': jax.random.normal(ks[2], (E,), jnp.float32) * s, 'wk': jax.random.normal(ks[3], (E, E), jnp.float32) * s, 'bk': jax.random.normal(ks[4], (E,), jnp.float32) * s, 'wv': jax.random.normal(ks[5], (E, E), jnp.float32) * s, 'bv': jax.random.normal(ks[6], (E,), jnp.float32) * s, 'wo': jax.random.normal(ks[7], (E, E), jnp.float32) * s, 'bo': jax.random.normal(ks[8], (E,), jnp.float32) * s}
    _L3_attn_all = _L3_attn_setup()
    _L3_attn_in = {k: v for k, v in _L3_attn_all.items() if k in ('wq', 'bq', 'wk', 'bk', 'wv', 'bv', 'wo', 'bo')}
    del _L3_attn_all

    def _L3_ffn_setup():
        import jax, jax.numpy as jnp
        import numpy as np
        N_EMBD = 192
        EXPERT_SIZES = [(8, 128), (8, 256)]
        TOP_K = 8
        NORM_TOPK_PROB = True
        EXPERT_WIDTHS = []
        for cnt, w in EXPERT_SIZES:
            EXPERT_WIDTHS += [w] * cnt
        EXPERT_OFFSETS = np.concatenate([[0], np.cumsum(EXPERT_WIDTHS)]).astype(np.int64)
        NUM_EXPERTS = len(EXPERT_WIDTHS)
        TOTAL_WIDTH = int(EXPERT_OFFSETS[-1])
        key = jax.random.key(seed)
        k1, k2, k3, k4 = jax.random.split(key, 4)
        x = jax.random.normal(k1, (1, 512, N_EMBD), dtype=jnp.float32)
        router_w = jax.random.normal(k2, (NUM_EXPERTS, N_EMBD), dtype=jnp.float32) * 0.02
        w1 = jnp.clip(jax.random.normal(k3, (N_EMBD, TOTAL_WIDTH), dtype=jnp.float32) * 0.02, -0.06, 0.06)
        w2 = jnp.clip(jax.random.normal(k4, (TOTAL_WIDTH, N_EMBD), dtype=jnp.float32) * 0.02, -0.06, 0.06)
        return {'x': x, 'router_w': router_w, 'w1': w1, 'w2': w2}
    _L3_ffn_all = _L3_ffn_setup()
    _L3_ffn_in = {k: v for k, v in _L3_ffn_all.items() if k in ('router_w', 'w1', 'w2')}
    del _L3_ffn_all
    return {'x': x, 'L0_tok_W': _L0_tok_in['W'], 'L0_tok_b': _L0_tok_in['b'], 'L0_tok_pos_emb': _L0_tok_in['pos_emb'], 'L0_attn_delay_weights': _L0_attn_in['delay_weights'], 'L0_attn_membrane_potentials': _L0_attn_in['membrane_potentials'], 'L0_attn_decay_constant': _L0_attn_in['decay_constant'], 'L0_attn_Wq': _L0_attn_in['Wq'], 'L0_attn_Wk': _L0_attn_in['Wk'], 'L0_attn_Wv': _L0_attn_in['Wv'], 'L0_attn_Wo': _L0_attn_in['Wo'], 'L0_attn_bo': _L0_attn_in['bo'], 'L0_ffn_router_w': _L0_ffn_in['router_w'], 'L0_ffn_router_b': _L0_ffn_in['router_b'], 'L0_ffn_expert_w': _L0_ffn_in['expert_w'], 'L0_ffn_expert_b': _L0_ffn_in['expert_b'], 'L1_attn_Wqkv': _L1_attn_in['Wqkv'], 'L1_attn_Wproj': _L1_attn_in['Wproj'], 'L1_attn_bproj': _L1_attn_in['bproj'], 'L1_attn_s_q': _L1_attn_in['s_q'], 'L1_attn_s_k': _L1_attn_in['s_k'], 'L1_attn_s_v': _L1_attn_in['s_v'], 'L1_attn_s_attn': _L1_attn_in['s_attn'], 'L1_attn_s_after': _L1_attn_in['s_after'], 'L1_ffn_attn_q': _L1_ffn_in['attn_q'], 'L1_ffn_attn_k': _L1_ffn_in['attn_k'], 'L1_ffn_attn_v': _L1_ffn_in['attn_v'], 'L1_ffn_attn_o': _L1_ffn_in['attn_o'], 'L1_ffn_ffn_wi': _L1_ffn_in['ffn_wi'], 'L1_ffn_ffn_wo': _L1_ffn_in['ffn_wo'], 'L1_ffn_ln1': _L1_ffn_in['ln1'], 'L1_ffn_ln2': _L1_ffn_in['ln2'], 'L1_ffn_ln_f': _L1_ffn_in['ln_f'], 'L1_ffn_rel_emb': _L1_ffn_in['rel_emb'], 'L1_ffn_gate_w': _L1_ffn_in['gate_w'], 'L1_ffn_moe_w1': _L1_ffn_in['moe_w1'], 'L1_ffn_moe_w2': _L1_ffn_in['moe_w2'], 'L2_attn_Wq': _L2_attn_in['Wq'], 'L2_attn_bq': _L2_attn_in['bq'], 'L2_attn_Wk': _L2_attn_in['Wk'], 'L2_attn_bk': _L2_attn_in['bk'], 'L2_attn_Wv': _L2_attn_in['Wv'], 'L2_attn_bv': _L2_attn_in['bv'], 'L2_attn_Wo': _L2_attn_in['Wo'], 'L2_attn_bo': _L2_attn_in['bo'], 'L2_ffn_Wr': _L2_ffn_in['Wr'], 'L2_ffn_W1': _L2_ffn_in['W1'], 'L2_ffn_b1': _L2_ffn_in['b1'], 'L2_ffn_W2': _L2_ffn_in['W2'], 'L2_ffn_b2': _L2_ffn_in['b2'], 'L3_attn_wq': _L3_attn_in['wq'], 'L3_attn_bq': _L3_attn_in['bq'], 'L3_attn_wk': _L3_attn_in['wk'], 'L3_attn_bk': _L3_attn_in['bk'], 'L3_attn_wv': _L3_attn_in['wv'], 'L3_attn_bv': _L3_attn_in['bv'], 'L3_attn_wo': _L3_attn_in['wo'], 'L3_attn_bo': _L3_attn_in['bo'], 'L3_ffn_router_w': _L3_ffn_in['router_w'], 'L3_ffn_w1': _L3_ffn_in['w1'], 'L3_ffn_w2': _L3_ffn_in['w2']}

def reference(x, L0_tok_W, L0_tok_b, L0_tok_pos_emb, L0_attn_delay_weights, L0_attn_membrane_potentials, L0_attn_decay_constant, L0_attn_Wq, L0_attn_Wk, L0_attn_Wv, L0_attn_Wo, L0_attn_bo, L0_ffn_router_w, L0_ffn_router_b, L0_ffn_expert_w, L0_ffn_expert_b, L1_attn_Wqkv, L1_attn_Wproj, L1_attn_bproj, L1_attn_s_q, L1_attn_s_k, L1_attn_s_v, L1_attn_s_attn, L1_attn_s_after, L1_ffn_attn_q, L1_ffn_attn_k, L1_ffn_attn_v, L1_ffn_attn_o, L1_ffn_ffn_wi, L1_ffn_ffn_wo, L1_ffn_ln1, L1_ffn_ln2, L1_ffn_ln_f, L1_ffn_rel_emb, L1_ffn_gate_w, L1_ffn_moe_w1, L1_ffn_moe_w2, L2_attn_Wq, L2_attn_bq, L2_attn_Wk, L2_attn_bk, L2_attn_Wv, L2_attn_bv, L2_attn_Wo, L2_attn_bo, L2_ffn_Wr, L2_ffn_W1, L2_ffn_b1, L2_ffn_W2, L2_ffn_b2, L3_attn_wq, L3_attn_bq, L3_attn_wk, L3_attn_bk, L3_attn_wv, L3_attn_bv, L3_attn_wo, L3_attn_bo, L3_ffn_router_w, L3_ffn_w1, L3_ffn_w2):
    import jax
    import jax.numpy as jnp

    def _L0_tok_ref(img, W, b, pos_emb):
        import jax, jax.numpy as jnp
        import numpy as np
        PATCH = 16
        B, H, Wd, C = img.shape
        ph, pw = (H // PATCH, Wd // PATCH)
        p = img.reshape(B, ph, PATCH, pw, PATCH, C)
        p = p.transpose(0, 1, 3, 2, 4, 5).reshape(B, ph * pw, PATCH * PATCH * C)
        out = jnp.einsum('bnk,kh->bnh', p, W) + b + pos_emb[None, :, :]
        return out

    def _L0_attn_ref(spikes, delay_weights, membrane_potentials, decay_constant, Wq, Wk, Wv, Wo, bo):
        import jax, jax.numpy as jnp
        import numpy as np
        B, S, E, H = (8, 512, 192, 1)
        HD = E // H
        LR = 0.01

        def _apply_delays(spikes, delay_weights):
            b, s, e = spikes.shape
            t = jnp.arange(s)
            src = t[:, None, None] - delay_weights[None, :, :]
            valid = src >= 0
            src_c = jnp.clip(src, 0, s - 1)
            g = spikes[:, src_c, jnp.arange(e)[None, None, :]]
            return jnp.sum(jnp.where(valid[None], g, jnp.float32(0)), axis=2)
        b, s, e = spikes.shape
        h, hd = (H, HD)
        delayed = _apply_delays(spikes, delay_weights)
        q = delayed @ Wq.T
        k = delayed @ Wk.T
        v = delayed @ Wv.T
        q = q.reshape(b, s, h, hd).transpose(0, 2, 1, 3)
        k = k.reshape(b, s, h, hd).transpose(0, 2, 1, 3)
        v = v.reshape(b, s, h, hd).transpose(0, 2, 1, 3)
        input_current = q.mean(axis=(0, 2))
        mp = jax.lax.stop_gradient(jnp.clip(decay_constant * membrane_potentials + LR * input_current, -2.0, 2.0))
        scores = jnp.einsum('bhqd,bhkd->bhqk', q, k) / np.sqrt(hd).astype(np.float32)
        mscores = jnp.einsum('bhqd,hd->bhq', q, mp)[..., None]
        attn = jax.nn.softmax(scores + 0.1 * mscores, axis=-1)
        out = jnp.einsum('bhqk,bhkd->bhqd', attn, v)
        out = out.transpose(0, 2, 1, 3).reshape(b, s, e)
        return out @ Wo.T + bo

    def _L0_ffn_ref(x, router_w, router_b, expert_w, expert_b):
        import jax, jax.numpy as jnp
        import numpy as np
        B, S, H = (4, 2048, 192)
        E, K = (8, 2)
        scores = jnp.einsum('bsh,eh->bse', x, router_w) + router_b
        probs = jax.nn.softmax(scores, axis=-1)
        top_probs, expert_ids = jax.lax.top_k(probs, K)
        y = jnp.einsum('bsh,edh->bsed', x, expert_w) + expert_b
        out_k = jnp.take_along_axis(y, expert_ids[..., None], axis=2)
        w = top_probs / (jnp.sum(top_probs, axis=-1, keepdims=True) + 1e-09)
        out = jnp.einsum('bsk,bskh->bsh', w, out_k)
        return out

    def _L1_attn_ref(x, Wqkv, Wproj, bproj, s_q, s_k, s_v, s_attn, s_after):
        import jax, jax.numpy as jnp
        import numpy as np
        LEVEL = 8
        NUM_HEADS = 12
        QN_SYM = float(-(LEVEL // 2))
        QP_SYM = float(LEVEL // 2 - 1)
        QN_ASYM = 0.0
        QP_ASYM = float(LEVEL - 1)

        def fake_quant(x, s, qn, qp):
            xc = jnp.clip(x / s, qn, qp)
            xr = xc + jax.lax.stop_gradient(jnp.round(xc) - xc)
            return s * xr
        B, N, C = x.shape
        H = NUM_HEADS
        D = C // H
        scale = D ** (-0.5)
        qkv = jnp.einsum('bnc,dc->bnd', x, Wqkv).reshape(B, N, 3, H, D).transpose(2, 0, 3, 1, 4)
        q, k, v = (qkv[0], qkv[1], qkv[2])
        q = fake_quant(q, s_q, QN_SYM, QP_SYM) * scale
        k = fake_quant(k, s_k, QN_SYM, QP_SYM)
        v = fake_quant(v, s_v, QN_SYM, QP_SYM)
        attn = jnp.einsum('bhnd,bhmd->bhnm', q, k)
        attn = fake_quant(attn / N, s_attn, QN_ASYM, QP_ASYM)
        out = jnp.einsum('bhnm,bhmd->bhnd', attn, v)
        out = fake_quant(out, s_after, QN_SYM, QP_SYM)
        out = out.transpose(0, 2, 1, 3).reshape(B, N, C)
        return out @ Wproj.T + bproj

    def _L1_ffn_ref(x, attn_q, attn_k, attn_v, attn_o, ffn_wi, ffn_wo, ln1, ln2, ln_f, rel_emb, gate_w, moe_w1, moe_w2):
        import jax, jax.numpy as jnp
        import numpy as np
        B, S, D, F = (2, 128, 192, 768)
        L, H, DK = (4, 12, 64)
        E, K = (8, 2)
        NB, MAXD = (32, 128)
        MOE_LAYERS = (1, 3)
        EPS = 1e-06

        def t5_layer_norm(x, w):
            var = jnp.mean(x * x, axis=-1, keepdims=True)
            return w * x * jax.lax.rsqrt(var + EPS)

        def relative_position_bias(rel_emb, seq_len):
            ctx = jnp.arange(seq_len)[:, None]
            mem = jnp.arange(seq_len)[None, :]
            rel = mem - ctx
            nb = NB // 2
            buckets = (rel > 0).astype(jnp.int32) * nb
            n = jnp.abs(rel)
            max_exact = nb // 2
            is_small = n < max_exact
            nf = jnp.maximum(n, 1).astype(jnp.float32)
            large = max_exact + (jnp.log(nf / max_exact) / np.log(MAXD / max_exact) * (nb - max_exact)).astype(jnp.int32)
            large = jnp.minimum(large, nb - 1)
            buckets = buckets + jnp.where(is_small, n, large)
            return rel_emb[buckets].transpose(2, 0, 1)[None]

        def moe_ffn(x2d, gw, w1, w2):
            logits = x2d @ gw
            vals, idx = jax.lax.top_k(logits, K)
            gsc = jax.nn.softmax(vals, axis=-1)
            T = x2d.shape[0]
            cw = jnp.zeros((T, E), x2d.dtype).at[jnp.arange(T)[:, None], idx].add(gsc)

            def body(acc, xs):
                w1e, w2e, cwe = xs
                y = jax.nn.gelu(x2d @ w1e, approximate=False) @ w2e
                return (acc + cwe[:, None] * y, None)
            out, _ = jax.lax.scan(body, jnp.zeros_like(x2d), (w1, w2, cw.T))
            return out
        b, s, d = x.shape
        bias = relative_position_bias(rel_emb, s)
        h = x
        mi = 0
        for i in range(L):
            nx = t5_layer_norm(h, ln1[i])
            q = (nx @ attn_q[i]).reshape(b, s, H, DK)
            k = (nx @ attn_k[i]).reshape(b, s, H, DK)
            v = (nx @ attn_v[i]).reshape(b, s, H, DK)
            scores = jnp.einsum('bqhd,bkhd->bhqk', q, k) + bias
            attn = jax.nn.softmax(scores, axis=-1)
            ctx = jnp.einsum('bhqk,bkhd->bqhd', attn, v).reshape(b, s, H * DK)
            h = h + ctx @ attn_o[i]
            nx = t5_layer_norm(h, ln2[i])
            y = jax.nn.relu(nx @ ffn_wi[i]) @ ffn_wo[i]
            if i in MOE_LAYERS:
                y = y + moe_ffn(nx.reshape(-1, d), gate_w[mi], moe_w1[mi], moe_w2[mi]).reshape(b, s, d)
                mi += 1
            h = h + y
        return t5_layer_norm(h, ln_f)

    def _L2_attn_ref(query, Wq, bq, Wk, bk, Wv, bv, Wo, bo):
        import jax, jax.numpy as jnp
        import numpy as np
        B, L, D, H = (2, 512, 192, 12)
        HD = D // H
        ROPE_BASE = 10000.0

        def apply_rope(x):
            d = x.shape[-1]
            pos = jnp.arange(x.shape[2], dtype=jnp.float32)
            inv_freq = 1.0 / ROPE_BASE ** (jnp.arange(0, d, 2, dtype=jnp.float32) / d)
            ang = pos[:, None] * inv_freq[None, :]
            cos = jnp.concatenate([jnp.cos(ang), jnp.cos(ang)], axis=-1)
            sin = jnp.concatenate([jnp.sin(ang), jnp.sin(ang)], axis=-1)
            x1, x2 = jnp.split(x, 2, axis=-1)
            rot = jnp.concatenate([-x2, x1], axis=-1)
            return x * cos[None, None, :, :].astype(x.dtype) + rot * sin[None, None, :, :].astype(x.dtype)
        b, l, _ = query.shape
        q = (query @ Wq.T + bq).reshape(b, l, H, HD).transpose(0, 2, 1, 3)
        k = (query @ Wk.T + bk).reshape(b, l, H, HD).transpose(0, 2, 1, 3)
        v = (query @ Wv.T + bv).reshape(b, l, H, HD).transpose(0, 2, 1, 3)
        q = apply_rope(q)
        k = apply_rope(k)
        scores = jnp.einsum('bhqd,bhkd->bhqk', q, k) / np.sqrt(HD).astype(np.float32)
        causal = jnp.triu(jnp.ones((l, l), dtype=bool), k=1)
        scores = jnp.where(causal[None, None, :, :], -jnp.inf, scores)
        attn = jax.nn.softmax(scores, axis=-1)
        out = jnp.einsum('bhqk,bhkd->bhqd', attn, v)
        out = out.transpose(0, 2, 1, 3).reshape(b, l, D)
        return out @ Wo.T + bo

    def _L2_ffn_ref(x, Wr, W1, b1, W2, b2):
        import jax, jax.numpy as jnp
        import numpy as np
        D_MODEL = 192
        N_EXPERTS = 16
        TOP_K = 2
        D_FF = 4 * D_MODEL
        B, L = (4, 512)
        logits = jnp.einsum('bld,ed->ble', x, Wr)
        probs = jax.nn.softmax(logits, axis=-1)
        top_p, top_idx = jax.lax.top_k(probs, TOP_K)
        gating = jnp.sum(jax.nn.one_hot(top_idx, N_EXPERTS, dtype=probs.dtype) * top_p[..., None], axis=-2)
        gate_e = jnp.moveaxis(gating, -1, 0)

        def step(y, params):
            W1e, b1e, W2e, b2e, ge = params
            h = jax.nn.gelu(jnp.einsum('bld,df->blf', x, W1e) + b1e, approximate=False)
            out = jnp.einsum('blf,fd->bld', h, W2e) + b2e
            return (y + ge[..., None] * out, None)
        y0 = jnp.zeros_like(x)
        y, _ = jax.lax.scan(step, y0, (W1, b1, W2, b2, gate_e))
        return x + y

    def _L3_attn_ref(hidden_states, wq, bq, wk, bk, wv, bv, wo, bo):
        import jax, jax.numpy as jnp
        import numpy as np
        EMBED_DIM = 192
        NUM_HEADS = 12
        HEAD_DIM = EMBED_DIM // NUM_HEADS
        MAX_WAVELENGTH = 10000.0
        ROPE_PERCENT = 0.5

        def p_rope(x, positions):
            rope_angles = int(ROPE_PERCENT * HEAD_DIM) // 2
            nope_angles = HEAD_DIM // 2 - rope_angles
            fraction = 2.0 * jnp.arange(rope_angles, dtype=x.dtype) / HEAD_DIM
            timescale = MAX_WAVELENGTH ** fraction
            timescale = jnp.concatenate([timescale, jnp.full((nope_angles,), jnp.inf, dtype=x.dtype)])
            sinusoid = positions[:, None] / timescale[None, :]
            sin, cos = (jnp.sin(sinusoid), jnp.cos(sinusoid))
            x1, x2 = jnp.split(x, 2, axis=-1)
            return jnp.concatenate([x1 * cos - x2 * sin, x2 * cos + x1 * sin], axis=-1)

        def _shape(x, B, S):
            return x.reshape(B, S, NUM_HEADS, HEAD_DIM).transpose(0, 2, 1, 3).reshape(B * NUM_HEADS, S, HEAD_DIM)
        B, T, E = hidden_states.shape
        scaling = HEAD_DIM ** (-0.5)
        q = (hidden_states @ wq.T + bq) * scaling
        k = hidden_states @ wk.T + bk
        v = hidden_states @ wv.T + bv
        q = _shape(q, B, T)
        k = _shape(k, B, T)
        v = _shape(v, B, T)
        positions = jnp.arange(T, dtype=hidden_states.dtype)
        k = p_rope(k, positions)
        q = p_rope(q, positions)
        attn = jnp.einsum('bqd,bkd->bqk', q, k)
        attn = jax.nn.softmax(attn, axis=-1)
        out = jnp.einsum('bqk,bkd->bqd', attn, v)
        out = out.reshape(B, NUM_HEADS, T, HEAD_DIM).transpose(0, 2, 1, 3).reshape(B, T, E)
        return out @ wo.T + bo

    def _L3_ffn_ref(x, router_w, w1, w2):
        import jax, jax.numpy as jnp
        import numpy as np
        N_EMBD = 192
        EXPERT_SIZES = [(8, 128), (8, 256)]
        TOP_K = 8
        NORM_TOPK_PROB = True
        EXPERT_WIDTHS = []
        for cnt, w in EXPERT_SIZES:
            EXPERT_WIDTHS += [w] * cnt
        EXPERT_OFFSETS = np.concatenate([[0], np.cumsum(EXPERT_WIDTHS)]).astype(np.int64)
        NUM_EXPERTS = len(EXPERT_WIDTHS)
        TOTAL_WIDTH = int(EXPERT_OFFSETS[-1])
        B, S, D = x.shape
        xt = x.reshape(-1, D)
        T = xt.shape[0]
        logits = jnp.einsum('td,ed->te', xt, router_w)
        probs = jax.nn.softmax(logits, axis=-1)
        topk_w, topk_idx = jax.lax.top_k(probs, TOP_K)
        if NORM_TOPK_PROB:
            topk_w = topk_w / jnp.sum(topk_w, axis=-1, keepdims=True)
        comb = jnp.zeros((T, NUM_EXPERTS), dtype=xt.dtype)
        comb = comb.at[jnp.arange(T)[:, None], topk_idx].add(topk_w)
        out = jnp.zeros_like(xt)
        for e in range(NUM_EXPERTS):
            off = int(EXPERT_OFFSETS[e])
            wd = EXPERT_WIDTHS[e]
            h = jax.nn.gelu(xt @ w1[:, off:off + wd])
            out = out + comb[:, e:e + 1] * (h @ w2[off:off + wd, :])
        return out.reshape(B, S, D)
    h = _L0_tok_ref(x, L0_tok_W, L0_tok_b, L0_tok_pos_emb)
    h = h + _L0_attn_ref(_layernorm(h, axis=-1), L0_attn_delay_weights, L0_attn_membrane_potentials, L0_attn_decay_constant, L0_attn_Wq, L0_attn_Wk, L0_attn_Wv, L0_attn_Wo, L0_attn_bo)
    h = h + _L0_ffn_ref(_layernorm(h, axis=-1), L0_ffn_router_w, L0_ffn_router_b, L0_ffn_expert_w, L0_ffn_expert_b)
    h = h + _L1_attn_ref(_layernorm(h, axis=-1), L1_attn_Wqkv, L1_attn_Wproj, L1_attn_bproj, L1_attn_s_q, L1_attn_s_k, L1_attn_s_v, L1_attn_s_attn, L1_attn_s_after)
    h = h + _L1_ffn_ref(_layernorm(h, axis=-1), L1_ffn_attn_q, L1_ffn_attn_k, L1_ffn_attn_v, L1_ffn_attn_o, L1_ffn_ffn_wi, L1_ffn_ffn_wo, L1_ffn_ln1, L1_ffn_ln2, L1_ffn_ln_f, L1_ffn_rel_emb, L1_ffn_gate_w, L1_ffn_moe_w1, L1_ffn_moe_w2)
    h = h + _L2_attn_ref(_layernorm(h, axis=-1), L2_attn_Wq, L2_attn_bq, L2_attn_Wk, L2_attn_bk, L2_attn_Wv, L2_attn_bv, L2_attn_Wo, L2_attn_bo)
    h = h + _L2_ffn_ref(_layernorm(h, axis=-1), L2_ffn_Wr, L2_ffn_W1, L2_ffn_b1, L2_ffn_W2, L2_ffn_b2)
    h = h + _L3_attn_ref(_layernorm(h, axis=-1), L3_attn_wq, L3_attn_bq, L3_attn_wk, L3_attn_bk, L3_attn_wv, L3_attn_bv, L3_attn_wo, L3_attn_bo)
    h = h + _L3_ffn_ref(_layernorm(h, axis=-1), L3_ffn_router_w, L3_ffn_w1, L3_ffn_w2)
    return h

_drawn_inputs = setup_inputs


def setup_inputs(seed=0):
    import zlib

    import numpy as np

    out = dict(_drawn_inputs(seed))
    spreads = {'L0_tok_b': (0.0, 0.1),
     'L0_attn_membrane_potentials': (0.0, 0.8),
     'L0_attn_bo': (0.0, 0.1),
     'L1_attn_bproj': (0.0, 0.1),
     'L1_ffn_ln1': (1.0, 0.6),
     'L1_ffn_ln2': (1.0, 0.573),
     'L1_ffn_ln_f': (1.0, 0.2)}
    factors = {'L1_ffn_rel_emb': 8.0,
     'L2_attn_Wq': 3.242,
     'L2_attn_bq': 8.0,
     'L2_attn_Wk': 3.07,
     'L2_attn_bk': 8.0,
     'L2_attn_bv': 4.954,
     'L2_attn_bo': 2.7,
     'L2_ffn_Wr': 4.722,
     'L2_ffn_W1': 4.598,
     'L2_ffn_b1': 8.0,
     'L2_ffn_W2': 4.311,
     'L2_ffn_b2': 8.0,
     'L3_attn_wq': 8.0,
     'L3_attn_bq': 8.0,
     'L3_attn_wk': 8.0,
     'L3_attn_bk': 8.0,
     'L3_attn_wv': 6.906,
     'L3_attn_bv': 8.0,
     'L3_attn_wo': 7.082,
     'L3_attn_bo': 8.0,
     'L3_ffn_router_w': 8.0,
     'L3_ffn_w1': 8.0,
     'L3_ffn_w2': 8.0}
    for name, (base, spread) in spreads.items():
        noise = np.random.default_rng([zlib.crc32(name.encode()), seed]).standard_normal(out[name].shape)
        drawn = base * np.exp(spread * noise) if base else spread * noise
        out[name] = jnp.asarray(drawn.astype(out[name].dtype))
    for name, factor in factors.items():
        out[name] = (out[name] * factor).astype(out[name].dtype)
    return out
```

```python
from contextlib import ExitStack

import concourse.bass as bass
from concourse import mybir
import numpy as np

ALU = mybir.AluOpType
ACT = mybir.ActivationFunctionType
F32 = mybir.dt.float32
BF16 = mybir.dt.bfloat16
I32 = mybir.dt.int32
AX_X = mybir.AxisListType.X

P = 128
BATCH, SEQ, DIM = 64, 16, 192
TOK = BATCH * SEQ
NT = TOK // P
CH = 96
HALF = 512
PATCH_CHUNKS = 8
FF = 768
FC = FF // P
HEADS = 12
HPU = 3
BIG = 2.0 ** 100
ROUND = 1.5 * 2.0 ** 23
S_RING, PT_RING, O_RING, P_RING = 3, 2, 3, 3
C_DECAY, C_SQ, C_SK, C_SV, C_SATTN, C_SAFTER = range(6)


class Kern:
    pass


def allocate(nc, ctx):
    k = Kern()
    k.nc = nc

    def sb(name, shape, dt=F32):
        return ctx.enter_context(nc.sbuf_tensor(name, shape, dt))

    def sem(name):
        return ctx.enter_context(nc.semaphore(name))

    k.bank = [ctx.enter_context(nc.psum_tensor(f"bank{i}", [P, HALF], F32)) for i in range(8)]

    k.h = sb("h", [P, NT, DIM])
    k.z = sb("z", [P, NT, DIM])
    k.xn = sb("xn", [P, NT, DIM])
    k.xT = sb("xT", [CH, 2, TOK])
    k.stats = sb("stats", [P, NT, 6])
    k.mv = sb("mv", [P, NT, 2])
    k.var = sb("var", [P, NT])
    k.std = sb("std", [P, NT])
    k.rstd = sb("rstd", [P, NT])
    k.lnw = sb("lnw", [CH, 2])
    k.ident = sb("ident", [P, P])
    k.identb = sb("identb", [P, P], BF16)
    k.blk = sb("blk", [P, HPU, P])
    k.maskb = sb("maskb", [P, HPU, P], BF16)
    k.causalb = sb("causalb", [P, HPU, P], BF16)
    k.headmask = sb("headmask", [CH, 2, 6])
    k.rope = sb("rope", [CH, 4, SEQ])
    k.before = [sb(f"before{n}", [P, n_e, n_e]) for n, n_e in enumerate((8, 16, 16))]
    k.scal = sb("scal", [P, 8])
    k.feat = sb("feat", [CH, 9, 2])
    k.bias = sb("bias", [P, DIM])
    k.logits = sb("logits", [P, NT, 16])
    k.ex = sb("ex", [P, NT, 16])
    k.cw = sb("cw", [P, NT, 16])
    k.cwT = sb("cwT", [16, TOK])
    k.bout = sb("bout", [16, DIM])
    k.rb = sb("rb", [P, 16])
    k.wr = sb("wr", [CH, 2, 16])
    k.red = sb("red", [P, 4, NT])
    k.nmax = sb("nmax", [P, 32, HPU])
    k.rsum = sb("rsum", [P, 32, HPU])
    k.rinv = sb("rinv", [P, 32, HPU])
    k.w1 = [sb(f"w1_{s}", [CH, 2, FF]) for s in range(2)]
    k.w2 = [sb(f"w2_{s}", [P, FC, DIM]) for s in range(2)]
    k.b1 = [sb(f"b1_{s}", [P, FC]) for s in range(2)]
    k.wA = sb("wA", [P, 6 * FF])

    names = ("loaded", "dve_step", "pool_step", "normed", "std_in", "std_out", "turned", "evacuated_a",
             "evacuated_v", "scores", "max_done", "exp_done", "p_turned", "pt_copied", "pv_done", "o_copied",
             "masked_k", "l1_done", "hid_step", "l2_done", "acc_step", "w_free0", "w_free1",
             "w_loaded0", "w_loaded1", "half_sum", "quant_a", "stored")
    k.sems = []
    for n in names:
        s = sem(n)
        k.sems.append(s)
    (k.loaded, k.dve_step, k.pool_step, k.normed, k.std_in, k.std_out, k.turned, k.evacuated_a,
     k.evacuated_v, k.scores, k.max_done, k.exp_done, k.p_turned, k.pt_copied, k.pv_done, k.o_copied,
     k.masked_k, k.l1_done, k.hid_step, k.l2_done, k.acc_step, w_free0, w_free1,
     w_loaded0, w_loaded1, k.half_sum, k.quant_a, k.stored) = k.sems
    k.w_free, k.w_loaded = [w_free0, w_free1], [w_loaded0, w_loaded1]
    nums = [s.num for s in k.sems]
    k.sem_range = range(min(nums), max(nums) + 1)
    assert len(k.sem_range) == len(nums)
    return k


def end_phase(k):
    k.nc.all_engine_barrier(sems_to_clear=k.sem_range)


def issue_loads(sp, k, loads):
    for dst, src in loads:
        sp.dma_start(dst, src).then_inc(k.loaded, 16)
    if loads:
        sp.wait_ge(k.loaded, 16 * len(loads))


def chain(eng, sem):
    count = [0]

    def link(ins, n=1):
        count[0] += 1
        ins.then_inc(sem, 1)
        eng.wait_ge(sem, count[0])

    return link


def load_phase(k, loads):
    with k.nc.Block(no_gpsimd_drain=True) as block:
        @block.sync
        def _(sp):
            issue_loads(sp, k, loads)
    end_phase(k)


def masks_phase(k, causal01):
    with k.nc.Block(no_gpsimd_drain=True) as block:
        @block.vector
        def _(dve):
            for j in range(HPU):
                dve.tensor_scalar(k.maskb[:, j, :], k.blk[:, j, :], -1.0, BIG, ALU.add, ALU.mult)
                dve.tensor_scalar(k.causalb[:, j, :], causal01[:], -1.0, BIG, ALU.add, ALU.mult)
            dve.tensor_copy(k.identb[:], k.ident[:])
    end_phase(k)



def embed_phase(k, patches, w, pos, loads):
    nc = k.nc
    with nc.Block(no_gpsimd_drain=True) as block:
        @block.sync
        def _(sp):
            issue_loads(sp, k, loads)

        @block.tensor
        def _(pe):
            for t in range(NT):
                for c in range(PATCH_CHUNKS):
                    mm = pe.matmul(k.bank[t][:, 0:DIM], patches[:, c, t * P:(t + 1) * P], w[:, c, :],
                                   start=(c == 0), stop=(c == PATCH_CHUNKS - 1))
                mm.then_inc(k.turned, 1)

        @block.vector
        def _(dve):
            link = chain(dve, k.dve_step)
            link(dve.tensor_tensor(pos[:], pos[:], k.bias[:], ALU.add))
            for t in range(NT):
                dve.wait_ge(k.turned, t + 1)
                dve.tensor_tensor(k.h[:, t, :], k.bank[t][:, 0:DIM], pos[:], ALU.add)
    end_phase(k)



def norm_stats(k, dve, link, src, eps, rms):
    for t in range(NT):
        last = dve.bn_stats(k.stats[:, t, :], src[:, t, :])
    link(last)
    for t in range(NT):
        last = dve.bn_aggr(k.mv[:, t, :], k.stats[:, t, :])
    link(last)
    mean, var = k.mv[:, :, 0], k.mv[:, :, 1]
    if rms:
        link(dve.tensor_tensor(k.var[:], mean, mean, ALU.mult))
        link(dve.tensor_tensor(k.var[:], k.var[:], var, ALU.add))
        dve.tensor_scalar(k.var[:], k.var[:], eps, None, ALU.add).then_inc(k.std_in, 1)
    else:
        dve.tensor_scalar(k.var[:], var, eps, None, ALU.add).then_inc(k.std_in, 1)
    dve.wait_ge(k.std_out, 1)
    link(dve.reciprocal(k.rstd[:], k.std[:]))


def norm_phase(k, src, eps, rms=False, dst=None, loads=()):
    nc = k.nc

    def out_T(c, n):
        return k.xT[:, c, n * HALF:(n + 1) * HALF] if dst is None else dst(c, n)

    def bank_of(c, n):
        b = k.bank[2 * n + c][0:CH, :]
        return b if dst is None else b.rearrange("p (b s) -> p b s", s=SEQ)

    with nc.Block(no_gpsimd_drain=True) as block:
        @block.sync
        def _(sp):
            issue_loads(sp, k, loads)

        @block.scalar
        def _(act):
            act.wait_ge(k.std_in, 1)
            act.activation(k.std[:], k.var[:], ACT.Sqrt).then_inc(k.std_out, 1)
            for n in range(2):
                act.wait_ge(k.turned, 4 * (n + 1))
                if rms:
                    act.activation(out_T(0, n), bank_of(0, n), ACT.Copy, scale=k.lnw[:, 0:1])
                else:
                    act.activation(out_T(0, n), bank_of(0, n), ACT.Copy)

        @block.vector
        def _(dve):
            link = chain(dve, k.dve_step)
            norm_stats(k, dve, link, src, eps, rms)
            for t in range(NT):
                if rms:
                    ins = dve.tensor_scalar(k.xn[:, t, :], src[:, t, :], k.rstd[:, t:t + 1], None, ALU.mult)
                else:
                    ins = dve.tensor_scalar(k.xn[:, t, :], src[:, t, :], k.mv[:, t, 0:1], k.rstd[:, t:t + 1],
                                            ALU.subtract, ALU.mult)
                ins.then_inc(k.normed, 1)
            for n in range(2):
                dve.wait_ge(k.turned, 4 * (n + 1))
                if rms:
                    dve.tensor_scalar(out_T(1, n), bank_of(1, n), k.lnw[:, 1:2], None, ALU.mult)
                else:
                    dve.tensor_copy(out_T(1, n), bank_of(1, n))

        @block.tensor
        def _(pe):
            for t in range(NT):
                pe.wait_ge(k.normed, t + 1)
                for c in range(2):
                    mm = pe.transpose(k.bank[2 * (t // 4) + c][0:CH, (t % 4) * P:(t % 4 + 1) * P],
                                      k.xn[:, t, c * CH:(c + 1) * CH], k.ident[:])
                mm.then_inc(k.turned, 1)
    end_phase(k)


def final_norm_phase(k, eps):
    with k.nc.Block(no_gpsimd_drain=True) as block:
        @block.scalar
        def _(act):
            act.wait_ge(k.std_in, 1)
            act.activation(k.std[:], k.var[:], ACT.Sqrt).then_inc(k.std_out, 1)

        @block.vector
        def _(dve):
            link = chain(dve, k.dve_step)
            norm_stats(k, dve, link, k.z, eps, True)
            for t in range(NT):
                last = dve.scalar_tensor_tensor(k.xn[:, t, :], k.z[:, t, :], k.rstd[:, t:t + 1], k.bias[:],
                                                ALU.mult, ALU.mult)
            link(last)
            dve.tensor_tensor(k.h[:], k.h[:], k.xn[:], ALU.add)
    end_phase(k)



def attention_phase(k, units, width, dim, units_per_bank, heads_in, score, masks, value, ctx_out, prep=None,
                    loads=()):
    nc = k.nc
    pbuf, ptbuf, kmask = k.pbuf, k.ptbuf, k.kmask
    n_banks = units // units_per_bank

    def s_bank(u):
        return k.bank[u % S_RING][:, 0:width * P]

    def pt_bank(u):
        return k.bank[S_RING + u % PT_RING][:, 0:width * P]

    def o_bank(b):
        return k.bank[S_RING + PT_RING + b % O_RING][:, 0:units_per_bank * width * dim]

    with nc.Block(no_gpsimd_drain=True) as block:
        @block.sync
        def _(sp):
            issue_loads(sp, k, loads)

        @block.gpsimd
        def _(pool):
            if prep is not None:
                for u in range(units):
                    if u >= 3:
                        pool.wait_ge(k.scores, u - 2)
                    prep(pool, u, kmask[u % 3]).then_inc(k.masked_k, 1)

        @block.tensor
        def _(pe):
            for s in range(units + 3):
                if s < units:
                    u = s
                    if u >= S_RING:
                        pe.wait_ge(k.exp_done, u - S_RING + 1)
                    if prep is not None:
                        pe.wait_ge(k.masked_k, u + 1)
                    for i, m in enumerate(masks(u)):
                        pe.matmul(s_bank(u), k.identb[:], m, start=(i == 0), stop=False)
                    score(pe, u, s_bank(u)).then_inc(k.scores, 1)
                u = s - 2
                if 0 <= u < units:
                    pe.wait_ge(k.exp_done, u + 1)
                    if u >= PT_RING:
                        pe.wait_ge(k.pt_copied, u - PT_RING + 1)
                    for j in range(width):
                        mm = pe.transpose(pt_bank(u)[:, j * P:(j + 1) * P],
                                          pbuf[u % P_RING][:, j * P:(j + 1) * P], k.ident[:])
                    mm.then_inc(k.p_turned, 1)
                u = s - 3
                if 0 <= u < units:
                    pe.wait_ge(k.pt_copied, u + 1)
                    b, at = u // units_per_bank, u % units_per_bank
                    if at == 0 and b >= O_RING:
                        pe.wait_ge(k.o_copied, b - O_RING + 1)
                    for j in range(width):
                        col = (at * width + j) * dim
                        mm = pe.matmul(o_bank(b)[:, col:col + dim], ptbuf[u % 2][:, j * P:(j + 1) * P],
                                       value(u, j), start=True, stop=True)
                    mm.then_inc(k.pv_done, 1)

        @block.scalar
        def _(act):
            for u in range(units):
                act.wait_ge(k.max_done, u + 1)
                if u >= P_RING:
                    act.wait_ge(k.p_turned, u - P_RING + 1)
                for j in range(width):
                    ins = act.activation(pbuf[u % P_RING][:, j * P:(j + 1) * P], s_bank(u)[:, j * P:(j + 1) * P],
                                         ACT.Exp, bias=k.nmax[:, u, j:j + 1], accum_out=k.rsum[:, u, j:j + 1])
                ins.then_inc(k.exp_done, 1)

        @block.vector
        def _(dve):
            link = chain(dve, k.dve_step)
            for s in range(units + 4):
                if s < units:
                    dve.wait_ge(k.scores, s + 1)
                    dve.tensor_reduce(k.nmax[:, s, 0:width], s_bank(s).rearrange("p (j q) -> p j q", j=width),
                                      AX_X, ALU.max, negate=True).then_inc(k.max_done, 1)
                u = s - 2
                if 0 <= u < units:
                    dve.wait_ge(k.p_turned, u + 1)
                    if u >= 2:
                        dve.wait_ge(k.pv_done, u - 1)
                    dve.tensor_copy(ptbuf[u % 2][:, 0:width * P], pt_bank(u)).then_inc(k.pt_copied, 1)
                u = s - 4
                if u >= 0 and u % units_per_bank == units_per_bank - 1:
                    b = u // units_per_bank
                    first = b * units_per_bank
                    link(dve.reciprocal(k.rinv[:, first:first + units_per_bank, 0:width],
                                        k.rsum[:, first:first + units_per_bank, 0:width]))
                    dve.wait_ge(k.pv_done, u + 1)
                    src, dst, inv = ctx_out(b, o_bank(b), k.rinv[:, first:first + units_per_bank, 0:width])
                    dve.tensor_tensor(dst, src, inv, ALU.mult).then_inc(k.o_copied, 1)
    end_phase(k)


def out_projection_phase(k, tiles, chunks, rows, ctx, w, dst, bias, loads=()):
    nc = k.nc
    per_bank = min(chunks, 3)
    nb = chunks // per_bank

    def turn_bank(i, c):
        return k.bank[(i % 2) * nb + c // per_bank][0:rows, (c % per_bank) * P:(c % per_bank + 1) * P]

    with nc.Block(no_gpsimd_drain=True) as block:
        @block.sync
        def _(sp):
            issue_loads(sp, k, loads)

        @block.gpsimd
        def _(pool):
            if bias is not None:
                for t in tiles:
                    pool.tensor_tensor(dst[:, t, :], dst[:, t, :], bias[:], ALU.add).then_inc(k.pool_step, 1)

        @block.tensor
        def _(pe):
            for i in range(len(tiles) + 1):
                if i < len(tiles):
                    if i >= 2:
                        pe.wait_ge(k.evacuated_a, i - 1)
                    for c in range(chunks):
                        mm = pe.transpose(turn_bank(i, c), ctx(tiles[i], c), k.ident[:])
                    mm.then_inc(k.turned, 1)
                if i >= 1:
                    n = i - 1
                    pe.wait_ge(k.evacuated_a, n + 1)
                    if n >= 2:
                        pe.wait_ge(k.evacuated_v, n - 1)
                    for c in range(chunks):
                        mm = pe.matmul(k.bank[4 + n % 2][:, 0:DIM], k.ctxT[n % 2][0:rows, c, :], w[0:rows, c, :],
                                       start=(c == 0), stop=(c == chunks - 1))
                    mm.then_inc(k.pv_done, 1)

        @block.scalar
        def _(act):
            for i in range(len(tiles)):
                act.wait_ge(k.turned, i + 1)
                if i >= 2:
                    act.wait_ge(k.pv_done, i - 1)
                for g in range(nb):
                    b = k.bank[(i % 2) * nb + g][0:rows, 0:per_bank * P]
                    ins = act.activation(k.ctxT[i % 2][0:rows, g * per_bank:(g + 1) * per_bank, :],
                                         b.rearrange("p (c q) -> p c q", q=P), ACT.Copy)
                ins.then_inc(k.evacuated_a, 1)

        @block.vector
        def _(dve):
            for i, t in enumerate(tiles):
                if bias is not None:
                    dve.wait_ge(k.pool_step, i + 1)
                dve.wait_ge(k.pv_done, i + 1)
                dve.tensor_tensor(dst[:, t, :], k.bank[4 + i % 2][:, 0:DIM], dst[:, t, :],
                                  ALU.add).then_inc(k.evacuated_v, 1)
    end_phase(k)


def head_prep(k, kT, quarter):
    def prep(pool, u, dst):
        t, g = u // 4, u % 4
        c, h0 = g // 2, HPU * (g % 2)
        keys = kT[:, c, t * P:(t + 1) * P].unsqueeze(1).broadcast_to([CH, HPU, P])
        mask = k.headmask[:, quarter, h0:h0 + HPU].unsqueeze(2).broadcast_to([CH, HPU, P])
        return pool.tensor_tensor(dst[:], keys, mask, ALU.mult)
    return prep


def narrow_heads_attention(k, qT, kT, v, maskb, ctx, loads=()):
    def score(pe, u, bank):
        t, g = u // 4, u % 4
        return pe.matmul(bank, qT[:, g // 2, t * P:(t + 1) * P], k.kmask[u % 3][:].rearrange("p j q -> p (j q)"),
                         start=False, stop=True)

    def value(u, j):
        t, head = u // 4, HPU * (u % 4) + j
        return v[:, t, head * 16:(head + 1) * 16]

    def ctx_out(b, bank, inv):
        return (bank.rearrange("p (h d) -> p h d", d=16), ctx[:, b, :].rearrange("p (h d) -> p h d", d=16),
                inv.rearrange("p u j -> p (u j)").unsqueeze(2).broadcast_to([P, HEADS, 16]))

    attention_phase(k, 4 * NT, HPU, 16, 4, None, score, lambda u: [maskb[:].rearrange("p j q -> p (j q)")],
                    value, ctx_out, head_prep(k, kT, 1), loads)


def rope_projection_phase(k, w, biases, rope, qT, kT, v, loads=()):
    nc = k.nc
    cos = k.rope[:, 2 * rope, :].unsqueeze(1).broadcast_to([CH, HALF // SEQ, SEQ])
    sin = k.rope[:, 2 * rope + 1, :].unsqueeze(1).broadcast_to([CH, HALF // SEQ, SEQ])
    jobs = [(which, m, n) for n in range(2) for which in range(2) for m in range(2)]

    def seqs(ap):
        return ap.rearrange("p (b s) -> p b s", s=SEQ)

    with nc.Block(no_gpsimd_drain=True) as block:
        @block.sync
        def _(sp):
            issue_loads(sp, k, loads)

        @block.tensor
        def _(pe):
            for i, (which, m, n) in enumerate(jobs):
                if i >= 4:
                    pe.wait_ge(k.evacuated_v, 2 * (i - 3))
                for s in range(2):
                    for c in range(2):
                        mm = pe.matmul(k.bank[2 * (i % 4) + s][0:CH, :],
                                       w[:, 2 * which + s, c, m * CH:(m + 1) * CH],
                                       k.xT[:, c, n * HALF:(n + 1) * HALF], start=(c == 0), stop=(c == 1))
                    mm.then_inc(k.turned, 1)
            for t in range(NT):
                if t % 2 == 0:
                    pe.wait_ge(k.evacuated_v, 2 * (len(jobs) - 3 + t // 2))
                for c in range(2):
                    mm = pe.matmul(k.bank[t][:, 0:DIM], k.xT[:, c, t * P:(t + 1) * P], w[:, 4, c, :],
                                   start=(c == 0), stop=(c == 1))
                mm.then_inc(k.turned, 1)

        @block.vector
        def _(dve):
            for i, (which, m, n) in enumerate(jobs):
                if i >= 2:
                    dve.wait_ge(k.pool_step, i - 1)
                for s, table in enumerate((cos, sin)):
                    dve.wait_ge(k.turned, 2 * i + s + 1)
                    dve.scalar_tensor_tensor(seqs(k.tmp[i % 2][0:CH, s, :]), seqs(k.bank[2 * (i % 4) + s][0:CH, :]),
                                             k.feat[:, biases + 2 * which + s, m:m + 1], table,
                                             ALU.add, ALU.mult).then_inc(k.evacuated_v, 1)
            for t in range(NT):
                dve.wait_ge(k.turned, 2 * len(jobs) + t + 1)
                dve.tensor_tensor(v[:, t, :], k.bank[t][:, 0:DIM], k.bias[:], ALU.add)

        @block.gpsimd
        def _(pool):
            for i, (which, m, n) in enumerate(jobs):
                pool.wait_ge(k.evacuated_v, 2 * i + 2)
                pool.tensor_tensor((qT, kT)[which][:, m, n * HALF:(n + 1) * HALF], k.tmp[i % 2][0:CH, 0, :],
                                   k.tmp[i % 2][0:CH, 1, :], ALU.add).then_inc(k.pool_step, 1)
    end_phase(k)



def delay_bits_phase(k, delays, mem):
    with k.nc.Block(no_gpsimd_drain=True) as block:
        @block.vector
        def _(dve):
            link = chain(dve, k.dve_step)
            s = k.shift
            link(dve.tensor_copy(s[:], delays[:]))
            link(dve.tensor_scalar(s[:], s[:], -1.0, float(SEQ), ALU.mult, ALU.add))
            link(dve.tensor_scalar(s[:], s[:], 0.0, 31.0, ALU.max, ALU.min))
            for i, step in enumerate((16, 8, 4, 2, 1)):
                link(dve.tensor_scalar(k.bit[:, i, :], s[:], float(step), None, ALU.is_ge))
                link(dve.scalar_tensor_tensor(s[:], k.bit[:, i, :], -float(step), s[:], ALU.mult, ALU.add))
                link(dve.tensor_scalar(k.nbit[:, i, :], k.bit[:, i, :], -1.0, 1.0, ALU.mult, ALU.add))
            for c in range(2):
                dve.memset(k.xe[:, c, :, 0:SEQ], 0.0)
                dve.tensor_copy(k.xe[:, c, :, 2 * SEQ:3 * SEQ],
                                k.xe[:, c, :, 2 * SEQ - 1:2 * SEQ].broadcast_to([CH, BATCH, SEQ]))
    end_phase(k)


def delay_phase(k, dT, loads):
    steps = (16, 8, 4, 2, 1)
    widths = (31, 23, 19, 17, 16)
    with k.nc.Block(no_gpsimd_drain=True) as block:
        @block.sync
        def _(sp):
            issue_loads(sp, k, loads)

        @block.scalar
        def _(act):
            for i in range(5):
                for c in range(2):
                    if i:
                        act.wait_ge(k.evacuated_v, 2 * (i - 1) + c + 1)
                    act.activation(k.moved[:, c, :, 0:widths[i]],
                                   k.xe[:, c, :, steps[i]:steps[i] + widths[i]], ACT.Copy,
                                   scale=k.bit[:, i, c:c + 1]).then_inc(k.evacuated_a, 1)

        @block.vector
        def _(dve):
            for i in range(5):
                for c in range(2):
                    dve.wait_ge(k.evacuated_a, 2 * i + c + 1)
                    stay = k.xe[:, c, :, 0:widths[i]]
                    out = stay if i < 4 else dT[:, c, :].rearrange("p (b s) -> p b s", s=SEQ)
                    dve.scalar_tensor_tensor(out, stay, k.nbit[:, i, c:c + 1], k.moved[:, c, :, 0:widths[i]],
                                             ALU.mult, ALU.add).then_inc(k.evacuated_v, 1)
    end_phase(k)


def l0_projection_phase(k, w, dT, qT, kT, v):
    jobs = [(which, m, n) for which in range(2) for m in range(2) for n in range(2)]
    with k.nc.Block(no_gpsimd_drain=True) as block:
        @block.tensor
        def _(pe):
            for i, (which, m, n) in enumerate(jobs):
                for c in range(2):
                    mm = pe.matmul(k.bank[i][0:CH, :], w[:, which, c, m * CH:(m + 1) * CH],
                                   dT[:, c, n * HALF:(n + 1) * HALF], start=(c == 0), stop=(c == 1))
                mm.then_inc(k.turned, 1)
            for t in range(NT):
                pe.wait_ge(k.evacuated_a, t // 2 + 1)
                for c in range(2):
                    mm = pe.matmul(k.bank[t // 2][:, (t % 2) * DIM:(t % 2 + 1) * DIM],
                                   dT[:, c, t * P:(t + 1) * P], w[:, 2, c, :], start=(c == 0), stop=(c == 1))
                mm.then_inc(k.turned, 1)

        @block.scalar
        def _(act):
            for i, (which, m, n) in enumerate(jobs):
                if i == 4:
                    act.wait_ge(k.half_sum, 1)
                act.wait_ge(k.turned, i + 1)
                src = k.bank[i][0:CH, :]
                if which == 0:
                    act.activation(qT[:, m, n * HALF:(n + 1) * HALF], src, ACT.Copy,
                                   accum_out=k.qsum[:, m, n:n + 1]).then_inc(k.evacuated_a, 1)
                else:
                    act.activation(kT[:, m, n * HALF:(n + 1) * HALF], src, ACT.Identity, scale=float(DIM ** -0.5),
                                   bias=k.mp[:, m:m + 1]).then_inc(k.evacuated_a, 1)

        @block.vector
        def _(dve):
            link = chain(dve, k.dve_step)
            dve.wait_ge(k.evacuated_a, 4)
            link(dve.tensor_reduce(k.mp[:], k.qsum[:], AX_X, ALU.add))
            link(dve.tensor_scalar(k.mp[:], k.mp[:], 0.01 / TOK, None, ALU.mult))
            link(dve.scalar_tensor_tensor(k.mp[:], k.feat[:, 0, :], k.scal[0:CH, C_DECAY:C_DECAY + 1], k.mp[:],
                                          ALU.mult, ALU.add))
            link(dve.tensor_scalar(k.mp[:], k.mp[:], -2.0, 2.0, ALU.max, ALU.min))
            dve.tensor_scalar(k.mp[:], k.mp[:], 0.1, None, ALU.mult).then_inc(k.half_sum, 1)
            for i in range(NT // 2):
                dve.wait_ge(k.turned, len(jobs) + 2 * i + 2)
                dve.tensor_copy(v[:, 2 * i:2 * i + 2, :].rearrange("p t d -> p (t d)"), k.bank[i][:, 0:2 * DIM])
    end_phase(k)


def l0_attention(k, qT, kT, v, ctx):
    def score(pe, u, bank):
        for j in range(2):
            t = 2 * u + j
            for c in range(2):
                mm = pe.matmul(bank[:, j * P:(j + 1) * P], qT[:, c, t * P:(t + 1) * P],
                               kT[:, c, t * P:(t + 1) * P], start=False, stop=(j == 1 and c == 1))
        return mm

    def ctx_out(b, bank, inv):
        return (bank.rearrange("p (t d) -> p t d", t=2), ctx[:, 2 * b:2 * b + 2, :],
                inv.rearrange("p u j -> p (u j)").unsqueeze(2).broadcast_to([P, 2, DIM]))

    attention_phase(k, NT // 2, 2, DIM, 1, None, score,
                    lambda u: [k.maskb[:, 0:2, :].rearrange("p j q -> p (j q)")],
                    lambda u, j: v[:, 2 * u + j, :], ctx_out)



def router_phase(k, n_e, top, norm, before, has_bias, want_T, loads=()):
    nc = k.nc
    lg, ex = k.logits[:, :, 0:n_e], k.ex[:, :, 0:n_e]
    cw = k.cw[:, :, 0:n_e]

    with nc.Block(no_gpsimd_drain=True) as block:
        @block.sync
        def _(sp):
            issue_loads(sp, k, loads)

        @block.tensor
        def _(pe):
            for t in range(NT):
                for c in range(2):
                    mm = pe.matmul(k.bank[0][:, t * n_e:(t + 1) * n_e], k.xT[:, c, t * P:(t + 1) * P],
                                   k.wr[:, c, 0:n_e], start=(c == 0), stop=(c == 1))
            mm.then_inc(k.turned, 1)
            if want_T:
                pe.wait_ge(k.normed, 1)
                for t in range(NT):
                    mm = pe.transpose(k.bank[1 + t // 4][0:n_e, (t % 4) * P:(t % 4 + 1) * P], cw[:, t, :],
                                      k.ident[:])
                mm.then_inc(k.turned, 1)

        @block.scalar
        def _(act):
            act.wait_ge(k.std_in, 1)
            act.activation(ex, ex, ACT.Exp).then_inc(k.std_out, 1)
            if want_T:
                act.wait_ge(k.turned, 2)
                for n in range(2):
                    act.activation(k.cwT[0:n_e, n * HALF:(n + 1) * HALF], k.bank[1 + n][0:n_e, :], ACT.Copy)

        @block.vector
        def _(dve):
            link = chain(dve, k.dve_step)
            dve.wait_ge(k.turned, 1)
            psum = k.bank[0][:, 0:NT * n_e].rearrange("p (t e) -> p t e", e=n_e)
            if has_bias:
                link(dve.tensor_tensor(lg, psum, k.rb[:, 0:n_e].unsqueeze(1).broadcast_to([P, NT, n_e]), ALU.add))
            else:
                link(dve.tensor_copy(lg, psum))
            link(dve.tensor_reduce(k.red[:, 0, :], lg, AX_X, ALU.max))
            dve.tensor_tensor(ex, lg, k.red[:, 0, :].unsqueeze(2).broadcast_to([P, NT, n_e]),
                              ALU.subtract).then_inc(k.std_in, 1)
            full = [P, NT, n_e, n_e]
            mine = lg.unsqueeze(3).broadcast_to(full)
            other = lg.unsqueeze(2).broadcast_to(full)
            earlier = before[:].unsqueeze(1).broadcast_to(full)
            a, b = (x[:].rearrange("p (t e f) -> p t e f", t=NT, f=n_e) for x in
                    (k.rank_a[:, 0:NT * n_e * n_e], k.rank_b[:, 0:NT * n_e * n_e]))
            dve.tensor_tensor(a, other, mine, ALU.is_gt)
            link(dve.tensor_tensor(b, other, mine, ALU.is_equal))
            link(dve.tensor_tensor(b, b, earlier, ALU.mult))
            link(dve.tensor_tensor(a, a, b, ALU.add))
            link(dve.tensor_reduce(cw, a, AX_X, ALU.add))
            dve.wait_ge(k.std_out, 1)
            link(dve.tensor_reduce(k.red[:, 1, :], ex, AX_X, ALU.add))
            link(dve.scalar_tensor_tensor(cw, cw, float(top), ex, ALU.is_lt, ALU.mult))
            if norm != "all":
                link(dve.tensor_reduce(k.red[:, 2, :], cw, AX_X, ALU.add))
            if norm == "probs":
                link(dve.scalar_tensor_tensor(k.red[:, 2, :], k.red[:, 1, :], 1e-9, k.red[:, 2, :],
                                              ALU.mult, ALU.add))
            den = k.red[:, 1, :] if norm == "all" else k.red[:, 2, :]
            link(dve.reciprocal(k.red[:, 3, :], den))
            dve.tensor_tensor(cw, cw, k.red[:, 3, :].unsqueeze(2).broadcast_to([P, NT, n_e]),
                              ALU.mult).then_inc(k.normed, 1)
    end_phase(k)


def linear_experts_phase(k, w, n_e, loads=()):
    pairs = n_e // 2
    with k.nc.Block(no_gpsimd_drain=True) as block:
        @block.sync
        def _(sp):
            issue_loads(sp, k, loads)

        @block.tensor
        def _(pe):
            i = 0
            for t in range(NT):
                for p in range(pairs + 1):
                    if i >= 8:
                        pe.wait_ge(k.evacuated_v, i - 7)
                    if p == 0:
                        mm = pe.matmul(k.bank[i % 8][:, 0:DIM], k.cwT[0:n_e, t * P:(t + 1) * P], k.bout[0:n_e, :],
                                       start=True, stop=True)
                    else:
                        for c in range(2):
                            mm = pe.matmul(k.bank[i % 8][:, 0:2 * DIM], k.xT[:, c, t * P:(t + 1) * P],
                                           w[:, c, (p - 1) * 2 * DIM:p * 2 * DIM], start=(c == 0), stop=(c == 1))
                    mm.then_inc(k.turned, 1)
                    i += 1

        @block.vector
        def _(dve):
            link = chain(dve, k.dve_step)
            i = 0
            for t in range(NT):
                for p in range(pairs + 1):
                    dve.wait_ge(k.turned, i + 1)
                    if p == 0:
                        link(dve.tensor_tensor(k.h[:, t, :], k.bank[i % 8][:, 0:DIM], k.h[:, t, :], ALU.add))
                    else:
                        for s in range(2):
                            e = 2 * (p - 1) + s
                            link(dve.scalar_tensor_tensor(k.h[:, t, :], k.bank[i % 8][:, s * DIM:(s + 1) * DIM],
                                                          k.cw[:, t, e:e + 1], k.h[:, t, :], ALU.mult, ALU.add))
                    dve.sem_inc(k.evacuated_v, 1)
                    i += 1
    end_phase(k)


def bias_experts_phase(k, n_e, add_xn, loads=()):
    with k.nc.Block(no_gpsimd_drain=True) as block:
        @block.sync
        def _(sp):
            issue_loads(sp, k, loads)

        @block.tensor
        def _(pe):
            for t in range(NT):
                pe.matmul(k.bank[t][:, 0:DIM], k.cwT[0:n_e, t * P:(t + 1) * P], k.bout[0:n_e, :],
                          start=True, stop=True).then_inc(k.turned, 1)

        @block.vector
        def _(dve):
            link = chain(dve, k.dve_step)
            link(dve.tensor_tensor(k.h[:], k.h[:], k.xn[:], ALU.add))
            for t in range(NT):
                dve.wait_ge(k.turned, t + 1)
                dve.tensor_tensor(k.h[:, t, :], k.bank[t][:, 0:DIM], k.h[:, t, :], ALU.add)
    end_phase(k)


def hidden_phase(k, n_e, func, dst, expert, groups=((0, 1, 2, 3, 4, 5),), weighted=True, use_b1=False, loads=()):
    nc = k.nc
    slots = min(2, n_e)
    rounds = n_e // slots
    units = 2 * slots
    n_g = len(groups)
    per_bank = min(n_g, 2)
    banks = 4 * (n_g // per_bank)
    n_loads = 3 if use_b1 else 2
    unit_steps = banks * per_bank
    start = 2 * unit_steps

    def first(pe, r, u):
        s, n = u // 2, u % 2
        if n == 0:
            pe.wait_ge(k.w_loaded[s], 16 + 16 * n_loads * r)
        for m in range(FC):
            g = (r * units + u) * FC + m
            pe.wait_ge(k.hid_step, g + 1)
            for c in range(2):
                mm = pe.matmul(k.bank[(u * FC + m) % 4][:], k.w1[s][:, c, m * P:(m + 1) * P],
                               k.xT[:, c, n * HALF:(n + 1) * HALF], start=(c == 0), stop=(c == 1))
            mm.then_inc(k.l1_done, 1)

    def second(pe, r, u):
        s = u // 2
        pe.wait_ge(k.hid_step, 4 + (r * units + u + 1) * FC)
        for t in range(4):
            for b in range(n_g // per_bank):
                i = t * (n_g // per_bank) + b
                pe.wait_ge(k.acc_step, start - 4 * per_bank + ((r * units + u) * banks + i + 1) * per_bank)
                for j in range(per_bank):
                    chunks = groups[b * per_bank + j]
                    for m in chunks:
                        mm = pe.matmul(k.bank[4 + (u * banks + i) % 4][:, j * DIM:(j + 1) * DIM],
                                       k.hT[u % 2][:, m, t * P:(t + 1) * P], k.w2[s][:, m, :],
                                       start=(m == chunks[0]), stop=(m == chunks[-1]))
                mm.then_inc(k.l2_done, 1)

    with nc.Block(no_gpsimd_drain=True) as block:
        @block.sync
        def _(sp):
            for s in range(slots):
                sp.sem_inc(k.w_loaded[s], 16)
            if rounds > 1:
                with sp.Fori(0, rounds - 1) as r:
                    for s in range(slots):
                        sp.wait_ge(k.acc_step, start + (r * units + 2 * (s + 1)) * unit_steps)
                        w1, w2, b1 = expert(2 * r + 2 + s)
                        sp.dma_start(k.w1[s][:], w1).then_inc(k.w_loaded[s], 16)
                        sp.dma_start(k.w2[s][:], w2).then_inc(k.w_loaded[s], 16)
                        if use_b1:
                            sp.dma_start(k.b1[s][:], b1).then_inc(k.w_loaded[s], 16)
            issue_loads(sp, k, loads)

        @block.tensor
        def _(pe):
            def body(r):
                first(pe, r, 0)
                for u in range(units):
                    if u + 1 < units:
                        first(pe, r, u + 1)
                    second(pe, r, u)
            if rounds > 1:
                with pe.Fori(0, rounds) as r:
                    body(r)
            else:
                body(0)

        @block.scalar
        def _(act):
            act.sem_inc(k.hid_step, 4)

            def body(r):
                for u in range(units):
                    act.wait_ge(k.acc_step, (r * units + u + 1) * unit_steps)
                    for m in range(FC):
                        act.wait_ge(k.l1_done, (r * units + u) * FC + m + 1)
                        src = k.bank[(u * FC + m) % 4][:]
                        if use_b1:
                            ins = act.activation(k.hT[u % 2][:, m, :], src, func, bias=k.b1[u // 2][:, m:m + 1])
                        else:
                            ins = act.activation(k.hT[u % 2][:, m, :], src, func)
                        ins.then_inc(k.hid_step, 1)
            if rounds > 1:
                with act.Fori(0, rounds) as r:
                    body(r)
            else:
                body(0)

        @block.vector
        def _(dve):
            dve.sem_inc(k.acc_step, start)

            def body(r):
                for u in range(units):
                    for t in range(4):
                        tile = 4 * (u % 2) + t
                        for b in range(n_g // per_bank):
                            i = t * (n_g // per_bank) + b
                            dve.wait_ge(k.l2_done, (r * units + u) * banks + i + 1)
                            for j in range(per_bank):
                                step = ((r * units + u) * banks + i) * per_bank + j
                                dve.wait_ge(k.acc_step, start + step - (3 if n_g == 1 else 0))
                                src = k.bank[4 + (u * banks + i) % 4][:, j * DIM:(j + 1) * DIM]
                                out = dst[:, tile, :]
                                if weighted:
                                    col = (slots * r + u // 2) * n_g + b * per_bank + j
                                    ins = dve.scalar_tensor_tensor(out, src, k.cw[:, tile, bass.ds(col, 1)], out,
                                                                   ALU.mult, ALU.add)
                                else:
                                    ins = dve.tensor_tensor(out, src, out, ALU.add)
                                ins.then_inc(k.acc_step, 1)
            if rounds > 1:
                with dve.Fori(0, rounds) as r:
                    body(r)
            else:
                body(0)
    end_phase(k)



def quant_projection_phase(k, w, qi, ki, vi, loads=()):
    jobs = [(which, m, n) for which in range(2) for m in range(2) for n in range(2)]
    total = len(jobs) + NT // 2

    def place(i):
        if i < len(jobs):
            which, m, n = jobs[i]
            return (k.bank[i % 8][0:CH, :], CH, HALF, C_SQ + which, (qi, ki)[which][:, m, n * HALF:(n + 1) * HALF])
        t = i - len(jobs)
        return (k.bank[i % 8][:, 0:2 * DIM], P, 2 * DIM, C_SV, vi[:, 2 * t:2 * t + 2, :].rearrange("p t d -> p (t d)"))

    with k.nc.Block(no_gpsimd_drain=True) as block:
        @block.sync
        def _(sp):
            issue_loads(sp, k, loads)

        @block.tensor
        def _(pe):
            for i in range(total):
                if i >= 8:
                    pe.wait_ge(k.evacuated_v, i - 7)
                bank = place(i)[0]
                if i < len(jobs):
                    which, m, n = jobs[i]
                    for c in range(2):
                        mm = pe.matmul(bank, w[:, c, which * DIM + m * CH:which * DIM + (m + 1) * CH],
                                       k.xT[:, c, n * HALF:(n + 1) * HALF], start=(c == 0), stop=(c == 1))
                else:
                    for j in range(2):
                        t = 2 * (i - len(jobs)) + j
                        for c in range(2):
                            mm = pe.matmul(bank[:, j * DIM:(j + 1) * DIM], k.xT[:, c, t * P:(t + 1) * P],
                                           w[:, c, 2 * DIM:3 * DIM], start=(c == 0), stop=(c == 1))
                mm.then_inc(k.turned, 1)

        @block.vector
        def _(dve):
            link = chain(dve, k.dve_step)
            link(dve.reciprocal(k.rscal[:], k.scal[:, 0:6]))
            for i in range(total):
                bank, rows, cols, col, _ = place(i)
                dve.wait_ge(k.turned, i + 1)
                if i >= 2:
                    dve.wait_ge(k.pool_step, i - 1)
                t = k.tmp[i % 2]
                dve.tensor_scalar(t[0:rows, 0, 0:cols], bank, k.rscal[0:rows, col:col + 1], -4.0,
                                  ALU.mult, ALU.max).then_inc(k.evacuated_v, 1)
                dve.wait_ge(k.evacuated_v, i + 1)
                dve.tensor_scalar(t[0:rows, 1, 0:cols], t[0:rows, 0, 0:cols], 3.0, ROUND,
                                  ALU.min, ALU.add).then_inc(k.quant_a, 1)

        @block.gpsimd
        def _(pool):
            for i in range(total):
                _, rows, cols, _, dst = place(i)
                pool.wait_ge(k.quant_a, i + 1)
                pool.tensor_scalar(dst, k.tmp[i % 2][0:rows, 1, 0:cols], -ROUND, None, ALU.add).then_inc(k.pool_step, 1)
    end_phase(k)


def quant_attention_phase(k, qi, ki, vi, ctx, loads=()):
    nc = k.nc
    units = 4 * NT
    with nc.Block(no_gpsimd_drain=True) as block:
        @block.sync
        def _(sp):
            issue_loads(sp, k, loads)

        @block.gpsimd
        def _(pool):
            for u in range(units):
                t, g = u // 4, u % 4
                h0 = HPU * (g % 2)
                if u >= 3:
                    pool.wait_ge(k.scores, u - 2)
                q = qi[:, g // 2, t * P:(t + 1) * P].unsqueeze(1).broadcast_to([CH, HPU, P])
                mask = k.headmask[:, 0, h0:h0 + HPU].unsqueeze(2).broadcast_to([CH, HPU, P])
                pool.tensor_tensor(k.kmaskb[u % 3][:], q, mask, ALU.mult).then_inc(k.masked_k, 1)

        @block.tensor
        def _(pe):
            for s in range(units + 2):
                if s < units:
                    t, g = s // 4, s % 4
                    pe.wait_ge(k.masked_k, s + 1)
                    if s >= 4:
                        pe.wait_ge(k.exp_done, s - 3)
                    pe.matmul(k.bank[s % 4][:, 0:HPU * P], ki[:, g // 2, t * P:(t + 1) * P],
                              k.kmaskb[s % 3][:].rearrange("p j q -> p (j q)"),
                              start=True, stop=True).then_inc(k.scores, 1)
                u = s - 2
                if u >= 0:
                    t, g = u // 4, u % 4
                    pe.wait_ge(k.pt_copied, u + 1)
                    if g == 0 and t >= 4:
                        pe.wait_ge(k.o_copied, t - 3)
                    for j in range(HPU):
                        head = HPU * g + j
                        mm = pe.matmul(k.bank[4 + t % 4][:, head * 16:(head + 1) * 16],
                                       k.attb[u % 3][:, j * P:(j + 1) * P],
                                       vi[:, t, head * 16:(head + 1) * 16], start=True, stop=True)
                    mm.then_inc(k.pv_done, 1)

        @block.scalar
        def _(act):
            act.wait_ge(k.half_sum, 1)
            for u in range(units):
                act.wait_ge(k.scores, u + 1)
                if u >= 2:
                    act.wait_ge(k.max_done, u - 1)
                act.activation(k.tmp[u % 2][:, 0, 0:HPU * P], k.bank[u % 4][:, 0:HPU * P], ACT.Copy,
                               scale=k.qscale[:, 0:1]).then_inc(k.exp_done, 1)

        @block.vector
        def _(dve):
            link = chain(dve, k.dve_step)
            sc = k.scal
            link(dve.tensor_scalar(k.qscale[:, 0:1], sc[:, C_SQ:C_SQ + 1], 0.25, sc[:, C_SK:C_SK + 1],
                                   ALU.mult, ALU.mult))
            link(dve.tensor_scalar(k.qscale[:, 0:1], k.qscale[:, 0:1], 1.0 / SEQ, None, ALU.mult))
            dve.tensor_tensor(k.qscale[:, 1:2], sc[:, C_SATTN:C_SATTN + 1], sc[:, C_SV:C_SV + 1],
                              ALU.mult).then_inc(k.half_sum, 1)
            dve.wait_ge(k.half_sum, 1)
            blk = k.blk[:].rearrange("p j q -> p (j q)")

            def quantise(u):
                a, b = k.tmp[u % 2][:, 0, 0:HPU * P], k.tmp[u % 2][:, 1, 0:HPU * P]
                dve.wait_ge(k.exp_done, u + 1)
                ins = dve.scalar_tensor_tensor(b, a, k.rscal[:, C_SATTN:C_SATTN + 1], blk, ALU.mult, ALU.mult)
                ins.then_inc(k.max_done, 1)
                dve.wait_ge(k.max_done, u + 1)
                link(dve.tensor_scalar(b, b, 0.0, 7.0, ALU.max, ALU.min))
                link(dve.tensor_scalar(b, b, ROUND, None, ALU.add))
                if u >= 3:
                    dve.wait_ge(k.pv_done, u - 2)
                dve.tensor_scalar(k.attb[u % 3][:], b, -ROUND, None, ALU.add).then_inc(k.pt_copied, 1)

            def output(t):
                o = ctx[:, t, :]
                dve.wait_ge(k.pv_done, 4 * (t + 1))
                link(dve.tensor_scalar(o, k.bank[4 + t % 4][:, 0:DIM], k.qscale[:, 1:2],
                                       k.rscal[:, C_SAFTER:C_SAFTER + 1], ALU.mult, ALU.mult))
                dve.sem_inc(k.o_copied, 1)
                link(dve.tensor_scalar(o, o, -4.0, 3.0, ALU.max, ALU.min))
                link(dve.tensor_scalar(o, o, ROUND, None, ALU.add))
                link(dve.tensor_scalar(o, o, -ROUND, sc[:, C_SAFTER:C_SAFTER + 1], ALU.add, ALU.mult))

            for u in range(units):
                quantise(u)
                if u % 4 == 2 and u > 4:
                    output(u // 4 - 1)
            output(NT - 1)
    end_phase(k)



def t5_bias_phase(k, bias16, full):
    with k.nc.Block(no_gpsimd_drain=True) as block:
        @block.vector
        def _(dve):
            link = chain(dve, k.dve_step)
            last = None
            mask = k.maskb[:, 0, :].rearrange("p (b s) -> p b s", s=SEQ)
            for head in range(HEADS):
                last = dve.tensor_tensor(full[:, head, :].rearrange("p (b s) -> p b s", s=SEQ), mask,
                                         bias16[:, head, :].unsqueeze(1).broadcast_to([P, P // SEQ, SEQ]), ALU.add)
            link(last)
            for i in range(3):
                link(dve.tensor_copy(k.t5_mask[:, i], full[:]))
                if i < 2:
                    link(dve.tensor_tensor(full[:], full[:], k.t5_mask[:, i], ALU.subtract))
    end_phase(k)


def t5_projection_phase(k, w, qT, kT, v, loads=()):
    jobs = [(which, m, n) for n in range(2) for which in range(2) for m in range(FC)]
    total = len(jobs) + 2 * NT
    with k.nc.Block(no_gpsimd_drain=True) as block:
        @block.sync
        def _(sp):
            issue_loads(sp, k, loads)

        @block.tensor
        def _(pe):
            for i in range(total):
                if i >= 8:
                    pe.wait_ge(k.evacuated_a if i % 2 == 0 else k.evacuated_v, (i - 8) // 2 + 1)
                if i < len(jobs):
                    which, m, n = jobs[i]
                    for c in range(2):
                        mm = pe.matmul(k.bank[i % 8][:], w[:, which, c, m * P:(m + 1) * P],
                                       k.xT[:, c, n * HALF:(n + 1) * HALF], start=(c == 0), stop=(c == 1))
                else:
                    t, b = (i - len(jobs)) // 2, i % 2
                    for c in range(2):
                        mm = pe.matmul(k.bank[i % 8][:, 0:FF // 2], k.xT[:, c, t * P:(t + 1) * P],
                                       w[:, 2, c, b * FF // 2:(b + 1) * FF // 2], start=(c == 0), stop=(c == 1))
                mm.then_inc(k.turned, 1)

        def evacuate(eng, parity, copy, done):
            for i in range(parity, total, 2):
                eng.wait_ge(k.turned, i + 1)
                if i < len(jobs):
                    which, m, n = jobs[i]
                    ins = copy((qT, kT)[which][:, m, n * HALF:(n + 1) * HALF], k.bank[i % 8][:])
                else:
                    t = (i - len(jobs)) // 2
                    ins = copy(v[:, t, parity * FF // 2:(parity + 1) * FF // 2], k.bank[i % 8][:, 0:FF // 2])
                ins.then_inc(done, 1)

        @block.scalar
        def _(act):
            evacuate(act, 0, lambda o, i: act.activation(o, i, ACT.Copy), k.evacuated_a)

        @block.vector
        def _(dve):
            evacuate(dve, 1, dve.tensor_copy, k.evacuated_v)
    end_phase(k)


def t5_attention(k, qT, kT, v, loads=()):
    def parts(u):
        t, half, odd = u // 4, u // 2 % 2, u % 2
        return t, 3 * half, odd

    def score(pe, u, bank):
        t, m0, odd = parts(u)
        for j in range(HPU):
            mm = pe.matmul(bank[:, j * P:(j + 1) * P], qT[64 * odd:64 * odd + 64, m0 + j, t * P:(t + 1) * P],
                           kT[64 * odd:64 * odd + 64, m0 + j, t * P:(t + 1) * P], start=False,
                           stop=(j == HPU - 1))
        return mm

    def masks(u):
        _, m0, odd = parts(u)
        first = 2 * m0 + odd
        return [k.t5_mask[:, i, first:first + 5:2, :] for i in range(3)]

    def value(u, j):
        t, m0, odd = parts(u)
        head = 2 * (m0 + j) + odd
        return v[:, t, head * 64:(head + 1) * 64]

    def ctx_out(b, bank, inv):
        t, m0 = b // 2, 3 * (b % 2)
        dst = qT[:, m0:m0 + 3, t * P:(t + 1) * P].rearrange("p m (o d) -> p o m d", o=2)
        return (bank.rearrange("p (o m d) -> p o m d", o=2, m=3), dst,
                inv.unsqueeze(3).broadcast_to([P, 2, 3, 64]))

    attention_phase(k, 4 * NT, HPU, 64, 2, None, score, masks, value, ctx_out, loads=loads)



def build(nc, a, out, stop=99):
    with ExitStack() as ctx:
        k = allocate(nc, ctx)

        def stage():
            return ExitStack()

        def tensor(stack, name, shape, dt=F32):
            return stack.enter_context(nc.sbuf_tensor(name, shape, dt))

        wA6 = k.wA[0:CH, 0:5 * 2 * DIM].rearrange("p (w c n) -> p w c n", w=5, c=2)
        woA = k.wA[0:CH, 5 * 2 * DIM:6 * 2 * DIM].rearrange("p (c n) -> p c n", c=2)

        def attention_loads(name, bias_name):
            return [(wA6, a[name][:, 0:5]), (woA, a[name][:, 5]), (k.bias[:], a[bias_name])]

        def expert_slots(w1, w2, b1, base=0):
            loads = []
            for s in range(2):
                loads += [(k.w1[s][:], w1(base + s)), (k.w2[s][:], w2(base + s))]
                if b1 is not None:
                    loads.append((k.b1[s][:], b1(base + s)))
            return loads

        with stage() as st:
            patches = tensor(st, "patches", [CH, PATCH_CHUNKS, TOK])
            wtok = tensor(st, "wtok", [CH, PATCH_CHUNKS, DIM])
            pos = tensor(st, "pos", [P, DIM])
            causal01 = tensor(st, "causal01", [P, P])
            load_phase(k, [(patches[:], a["patches"]), (wtok[:], a["wtok"]), (pos[:], a["pos"]),
                           (k.bias[:], a["btok"]), (k.ident[:], a["ident"]), (k.blk[:], a["blk"]),
                           (causal01[:], a["causal"]), (k.headmask[:], a["headmask"]), (k.rope[:], a["rope"]),
                           (k.before[0][:], a["before8"]), (k.before[1][:], a["before16"]),
                           (k.before[2][:], a["before16p"]), (k.scal[:], a["scal"]), (k.feat[:], a["feat"]),
                           (k.wr[:, :, 0:8], a["l0_wr"]), (k.rb[:, 0:8], a["l0_rb"])])
            masks_phase(k, causal01)
            embed_phase(k, patches, wtok, pos, [(wA6[:, 0:3], a["l0_w"][:, 0:3]), (woA, a["l0_w"][:, 3])])

        with stage() as st:
            dT = tensor(st, "dT", [CH, 2, TOK])
            with stage() as sub:
                k.xe = tensor(sub, "xe", [CH, 2, BATCH, 3 * SEQ])
                k.moved = tensor(sub, "moved", [CH, 2, BATCH, 31])
                k.shift = tensor(sub, "shift", [CH, 2])
                k.bit = tensor(sub, "bit", [CH, 5, 2])
                k.nbit = tensor(sub, "nbit", [CH, 5, 2])
                delays = tensor(sub, "delays", [CH, 2], I32)
                norm_phase(k, k.h, 1e-5, dst=lambda c, n: k.xe[:, c, 32 * n:32 * n + 32, SEQ:2 * SEQ],
                           loads=[(delays[:], a["delays"]), (k.bias[:], a["l0_bo"])])
                delay_bits_phase(k, delays, None)
                delay_phase(k, dT, [])
            with stage() as sub:
                qT = tensor(sub, "l0_qT", [CH, 2, TOK])
                kT = tensor(sub, "l0_kT", [CH, 2, TOK])
                v = tensor(sub, "l0_v", [P, NT, DIM])
                ctx_ = tensor(sub, "l0_ctx", [P, NT, DIM])
                k.qsum = tensor(sub, "qsum", [CH, 2, 2])
                k.mp = tensor(sub, "mp", [CH, 2])
                k.pbuf = [tensor(sub, f"l0_p{i}", [P, 2 * P]) for i in range(P_RING)]
                k.ptbuf = [tensor(sub, f"l0_pt{i}", [P, 2 * P]) for i in range(2)]
                k.ctxT = [tensor(sub, f"l0_ctxT{i}", [P, 2, P]) for i in range(2)]
                k.kmask = None
                l0_projection_phase(k, wA6, dT, qT, kT, v)
                l0_attention(k, qT, kT, v, ctx_)
                out_projection_phase(k, list(range(NT)), 2, CH, lambda t, c: ctx_[:, t, c * CH:(c + 1) * CH],
                                     woA, k.h, k.bias)
        if stop <= 1:
            return store(k, out)

        with stage() as st:
            we = tensor(st, "l0_we", [CH, 2, 8 * DIM])
            k.rank_a = tensor(st, "rank_a0", [P, NT * 64])
            k.rank_b = tensor(st, "rank_b0", [P, NT * 64])
            norm_phase(k, k.h, 1e-5, loads=[(we[:], a["l0_we"]), (k.bout[0:8, :], a["l0_be"])])
            router_phase(k, 8, 2, "probs", k.before[0], True, True)
            linear_experts_phase(k, we, 8, loads=[(k.wA[0:CH, 0:2 * 3 * DIM].rearrange("p (c n) -> p c n", c=2),
                                                   a["l1_wqkv"]), (woA, a["l1_wproj"]), (k.bias[:], a["l1_bo"])])
        if stop <= 2:
            return store(k, out)

        with stage() as st:
            qi = tensor(st, "qi", [CH, 2, TOK], BF16)
            ki = tensor(st, "ki", [CH, 2, TOK], BF16)
            vi = tensor(st, "vi", [P, NT, DIM], BF16)
            ctx_ = tensor(st, "l1_ctx", [P, NT, DIM])
            k.rscal = tensor(st, "rscal", [P, 6])
            k.qscale = tensor(st, "qscale", [P, 2])
            k.tmp = [tensor(st, f"l1_tmp{i}", [P, 2, HALF]) for i in range(2)]
            k.kmaskb = [tensor(st, f"kmaskb{i}", [CH, HPU, P], BF16) for i in range(3)]
            k.attb = [tensor(st, f"attb{i}", [P, HPU * P], BF16) for i in range(3)]
            k.ctxT = [tensor(st, f"l1_ctxT{i}", [P, 2, P]) for i in range(2)]
            norm_phase(k, k.h, 1e-5)
            quant_projection_phase(k, k.wA[0:CH, 0:2 * 3 * DIM].rearrange("p (c n) -> p c n", c=2), qi, ki, vi)
            quant_attention_phase(k, qi, ki, vi, ctx_)
            out_projection_phase(k, list(range(NT)), 2, CH, lambda t, c: ctx_[:, t, c * CH:(c + 1) * CH],
                                 woA, k.h, k.bias)
        if stop <= 3:
            return store(k, out)

        wqkv = k.wA[0:CH, 0:6 * FF].rearrange("p (w c n) -> p w c n", w=3, c=2)

        with stage() as st:
            norm_phase(k, k.h, 1e-5)
            k.t5_mask = tensor(st, "t5_mask", [P, 3, HEADS, P], BF16)
            wo5 = tensor(st, "wo5", [P, FC, DIM])
            with stage() as sub:
                bias16 = tensor(sub, "bias16", [P, HEADS, SEQ])
                full = tensor(sub, "full", [P, HEADS, P])
                load_phase(k, [(bias16[:], a["t5_bias16"])])
                t5_bias_phase(k, bias16, full)
            t5_start_phase(k)
            with nc.Fori(0, 2) as r:
                for j in range(2):
                    layer = 2 * r + j
                    with stage() as sub:
                        qT = tensor(sub, f"t5_qT{j}", [P, FC, TOK])
                        kT = tensor(sub, f"t5_kT{j}", [P, FC, TOK])
                        k.pbuf = [tensor(sub, f"t5_p{j}{i}", [P, HPU * P]) for i in range(P_RING)]
                        k.ptbuf = [tensor(sub, f"t5_pt{j}{i}", [P, HPU * P]) for i in range(2)]
                        k.kmask = None
                        v = tensor(sub, f"t5_v{j}", [P, NT, FF])
                        load_phase(k, [(wqkv, a["t5_wqkv"][layer]), (wo5[:], a["t5_wo"][layer]),
                                       (k.lnw[:], a["t5_ln1"][layer])])
                        norm_phase(k, k.z, 1e-6, rms=True)
                        t5_projection_phase(k, wqkv, qT, kT, v)
                        t5_attention(k, qT, kT, v,
                                     loads=[(k.w1[0][:], a["t5_wi"][layer]), (k.w2[0][:], a["t5_wo2"][layer]),
                                            (k.lnw[:], a["t5_ln2"][layer])])
                        k.ctxT = [kT[:, i, 0:FC * P].rearrange("p (c q) -> p c q", q=P)
                                  for i in range(2)]
                        out_projection_phase(k, list(range(NT)), FC, P, lambda t, c: qT[:, c, t * P:(t + 1) * P],
                                             wo5, k.z, None)
                    with stage() as sub:
                        k.hT = [tensor(sub, f"t5_hT{j}{i}", [P, FC, HALF]) for i in range(2)]
                        k.rank_a = tensor(sub, f"t5_ra{j}", [P, NT * 64])
                        k.rank_b = tensor(sub, f"t5_rb{j}", [P, NT * 64])
                        norm_phase(k, k.z, 1e-6, rms=True,
                                   loads=[(k.wr[:, :, 0:8], a["t5_gate"][r])] if j == 1 else [])
                        hidden_phase(k, 1, ACT.Relu, k.z, None, weighted=False)
                        if j == 1:
                            router_phase(k, 8, 2, "top", k.before[0], False, False,
                                         loads=expert_slots(lambda e: a["t5_moe1"][r * 8 + e],
                                                            lambda e: a["t5_moe2"][r * 8 + e], None))
                            hidden_phase(k, 8, ACT.Gelu, k.z,
                                         lambda e: (a["t5_moe1"][r * 8 + e], a["t5_moe2"][r * 8 + e], None))
            load_phase(k, [(k.bias[:], a["t5_lnf"])])
            final_norm_phase(k, 1e-6)
        if stop <= 4:
            return store(k, out)

        for level in (2, 3):
            with stage() as st:
                qT = tensor(st, f"l{level}_qT", [CH, 2, TOK])
                kT = tensor(st, f"l{level}_kT", [CH, 2, TOK])
                v = tensor(st, f"l{level}_v", [P, NT, DIM])
                ctx_ = tensor(st, f"l{level}_ctx", [P, NT, DIM])
                k.tmp = [tensor(st, f"l{level}_tmp{i}", [P, 2, HALF]) for i in range(2)]
                k.pbuf = [tensor(st, f"l{level}_p{i}", [P, HPU * P]) for i in range(P_RING)]
                k.ptbuf = [tensor(st, f"l{level}_pt{i}", [P, HPU * P]) for i in range(2)]
                k.kmask = [tensor(st, f"l{level}_km{i}", [CH, HPU, P]) for i in range(3)]
                k.ctxT = [tensor(st, f"l{level}_ctxT{i}", [P, 2, P]) for i in range(2)]
                norm_phase(k, k.h, 1e-5, loads=attention_loads(f"l{level}_w", f"l{level}_bv"))
                rope_projection_phase(k, wA6, 1 + 4 * (level - 2), level - 2, qT, kT, v)
                narrow_heads_attention(k, qT, kT, v, k.causalb if level == 2 else k.maskb, ctx_,
                                       loads=[(k.bias[:], a[f"l{level}_bo"]), (k.wr[:], a[f"l{level}_wr"])]
                                       + ([(k.bout[:], a["l2_b2"])] if level == 2 else []))
                out_projection_phase(k, list(range(NT)), 2, CH, lambda t, c: ctx_[:, t, c * CH:(c + 1) * CH],
                                     woA, k.h, k.bias)
            if stop <= 2 * level + 1:
                return store(k, out)
            with stage() as st:
                with stage() as sub:
                    k.rank_a = tensor(sub, f"rank_a{level}", [P, NT * 256])
                    k.rank_b = tensor(sub, f"rank_b{level}", [P, NT * 256])
                    if level == 2:
                        norm_phase(k, k.h, 1e-5,
                                   loads=expert_slots(lambda e: a["l2_w1"][e], lambda e: a["l2_w2"][e],
                                                      lambda e: a["l2_b1"][e]))
                        router_phase(k, 16, 2, "all", k.before[1], False, True)
                    else:
                        norm_phase(k, k.h, 1e-5,
                                   loads=expert_slots(lambda e: a["l3_w1"][e], lambda e: a["l3_w2"][e], None))
                        router_phase(k, 16, 8, "top", k.before[2], False, False)
                k.hT = [tensor(st, f"l{level}_hT{i}", [P, FC, HALF]) for i in range(2)]
                if level == 2:
                    bias_experts_phase(k, 16, True)
                    hidden_phase(k, 16, ACT.Gelu, k.h, lambda e: (a["l2_w1"][e], a["l2_w2"][e], a["l2_b1"][e]),
                                 use_b1=True)
                else:
                    hidden_phase(k, 4, ACT.Gelu_apprx_tanh, k.h, lambda e: (a["l3_w1"][e], a["l3_w2"][e], None),
                                 groups=((0,), (1,), (2, 3), (4, 5)))
            if level == 3 or stop <= 2 * level + 2:
                return store(k, out)


def t5_start_phase(k):
    with k.nc.Block(no_gpsimd_drain=True) as block:
        @block.vector
        def _(dve):
            dve.tensor_copy(k.z[:], k.xn[:])
    end_phase(k)


def store(k, out):
    with k.nc.Block(no_gpsimd_drain=True) as block:
        @block.sync
        def _(sp):
            sp.dma_start(out, k.h[:]).then_inc(k.stored, 16)
            sp.wait_ge(k.stored, 16)



def k_major(w):
    w = np.asarray(w)
    return w.reshape(2, CH, -1).transpose(1, 0, 2)


def swap_halves(w):
    w = np.asarray(w)
    return w.reshape(HEADS, 2, 8, -1)[:, ::-1].reshape(w.shape)


def hidden_major(w):
    return np.asarray(w).reshape(FC, P, DIM).transpose(1, 0, 2)


def rows(v):
    v = np.asarray(v).reshape(1, -1)
    return np.repeat(v, P, axis=0)


def columns(v):
    return np.asarray(v).reshape(2, CH).T


def lay_out(i):
    i = {n: np.asarray(v) for n, v in i.items()}
    a = {}
    x = i["x"].reshape(BATCH, 4, 16, 4, 16, 3).transpose(2, 4, 5, 0, 1, 3).reshape(PATCH_CHUNKS, CH, TOK)
    a["patches"] = x.transpose(1, 0, 2)
    a["wtok"] = i["L0_tok_W"].reshape(PATCH_CHUNKS, CH, DIM).transpose(1, 0, 2)
    a["pos"] = np.concatenate([i["L0_tok_pos_emb"]] * (P // SEQ), axis=0)
    a["btok"] = rows(i["L0_tok_b"])

    n = np.arange(P)
    same = (n[:, None] // SEQ == n[None, :] // SEQ)
    a["ident"] = np.eye(P, dtype=np.float32)
    a["blk"] = np.repeat(same.astype(np.float32)[:, None, :], HPU, axis=1)
    a["causal"] = (same & (n[None, :] <= n[:, None])).astype(np.float32)
    head = (np.arange(CH)[:, None] // 16 == np.arange(6)[None, :]).astype(np.float32)
    a["headmask"] = np.stack([head, head * np.float32(0.25)], axis=1)
    pos = np.arange(SEQ, dtype=np.float32)
    inv2 = (1.0 / 10000.0 ** (np.arange(0, 16, 2, dtype=np.float32) / 16)).astype(np.float32)
    ang2 = pos[None, :] * inv2[:, None]
    scale3 = (10000.0 ** (2.0 * np.arange(4, dtype=np.float32) / 16)).astype(np.float32)
    ang3 = np.concatenate([pos[None, :] / scale3[:, None], np.zeros((4, SEQ), np.float32)])
    tables = []
    for ang in (ang2, ang3):
        c, s = np.cos(ang), np.sin(ang)
        tables += [np.tile(np.concatenate([c, c]), (6, 1)), np.tile(np.concatenate([-s, s]), (6, 1))]
    a["rope"] = np.stack(tables, axis=1).astype(np.float32)
    order = [e for p in range(4) for e in (2 * p, 2 * p + 1, 8 + 2 * p, 9 + 2 * p)]
    for name, idx in (("before8", np.arange(8)), ("before16", np.arange(16)), ("before16p", np.array(order))):
        m = (idx[None, :] < idx[:, None]).astype(np.float32)
        a[name] = np.repeat(m[None], P, axis=0)

    z = np.zeros(1, np.float32)
    scal = [i["L0_attn_decay_constant"], i["L1_attn_s_q"], i["L1_attn_s_k"], i["L1_attn_s_v"],
            i["L1_attn_s_attn"], i["L1_attn_s_after"], z, z]
    a["scal"] = rows(np.concatenate([s.reshape(1) for s in scal]))
    feat = [i["L0_attn_membrane_potentials"].reshape(DIM)]
    for bq, bk in ((i["L2_attn_bq"], i["L2_attn_bk"]), (i["L3_attn_bq"], i["L3_attn_bk"])):
        feat += [bq, swap_halves(bq), bk, swap_halves(bk)]
    a["feat"] = np.stack([columns(f) for f in feat], axis=1)

    a["delays"] = columns(i["L0_attn_delay_weights"].reshape(DIM))
    a["l0_w"] = np.stack([k_major(i[f"L0_attn_W{c}"].T) for c in "qkvo"], axis=1)
    a["l0_bo"] = rows(i["L0_attn_bo"])
    a["l0_wr"] = k_major(i["L0_ffn_router_w"].T)
    a["l0_rb"] = rows(i["L0_ffn_router_b"])
    a["l0_we"] = k_major(i["L0_ffn_expert_w"].transpose(2, 0, 1).reshape(DIM, 8 * DIM))
    a["l0_be"] = i["L0_ffn_expert_b"]

    a["l1_wqkv"] = k_major(i["L1_attn_Wqkv"].T)
    a["l1_wproj"] = k_major(i["L1_attn_Wproj"].T)
    a["l1_bo"] = rows(i["L1_attn_bproj"])

    q = np.arange(SEQ)
    rel = q[None, :] - q[:, None]
    dist = np.abs(rel)
    large = 8 + (np.log(np.maximum(dist, 1).astype(np.float32) / 8) / np.log(16) * 8).astype(np.int32)
    bucket = (rel > 0) * 16 + np.where(dist < 8, dist, np.minimum(large, 15))
    a["t5_bias16"] = np.concatenate([i["L1_ffn_rel_emb"][bucket].transpose(0, 2, 1)] * (P // SEQ), axis=0)
    a["t5_wqkv"] = np.stack([np.stack([k_major(i[f"L1_ffn_attn_{c}"][l]) for c in "qkv"], axis=1) for l in range(4)])
    a["t5_wo"] = np.stack([hidden_major(i["L1_ffn_attn_o"][l]) for l in range(4)])
    a["t5_wi"] = np.stack([k_major(i["L1_ffn_ffn_wi"][l]) for l in range(4)])
    a["t5_wo2"] = np.stack([hidden_major(i["L1_ffn_ffn_wo"][l]) for l in range(4)])
    a["t5_ln1"] = np.stack([columns(i["L1_ffn_ln1"][l]) for l in range(4)])
    a["t5_ln2"] = np.stack([columns(i["L1_ffn_ln2"][l]) for l in range(4)])
    a["t5_lnf"] = rows(i["L1_ffn_ln_f"])
    a["t5_gate"] = np.stack([k_major(i["L1_ffn_gate_w"][m]) for m in range(2)])
    a["t5_moe1"] = np.stack([k_major(i["L1_ffn_moe_w1"][m, e]) for m in range(2) for e in range(8)])
    a["t5_moe2"] = np.stack([hidden_major(i["L1_ffn_moe_w2"][m, e]) for m in range(2) for e in range(8)])

    for lv, low in ((2, False), (3, True)):
        w = {c: i[f"L{lv}_attn_" + ("w" if low else "W") + c] for c in "qkvo"}
        mats = [w["q"].T, swap_halves(w["q"]).T, w["k"].T, swap_halves(w["k"]).T, w["v"].T, w["o"].T]
        a[f"l{lv}_w"] = np.stack([k_major(m) for m in mats], axis=1)
        a[f"l{lv}_bv"] = rows(i[f"L{lv}_attn_bv"])
        a[f"l{lv}_bo"] = rows(i[f"L{lv}_attn_bo"])
    a["l2_wr"] = k_major(i["L2_ffn_Wr"].T)
    a["l2_w1"] = np.stack([k_major(w) for w in i["L2_ffn_W1"]])
    a["l2_w2"] = np.stack([hidden_major(w) for w in i["L2_ffn_W2"]])
    a["l2_b1"] = i["L2_ffn_b1"].reshape(16, FC, P).transpose(0, 2, 1)
    a["l2_b2"] = i["L2_ffn_b2"]

    a["l3_wr"] = k_major(i["L3_ffn_router_w"][np.array(order)].T)
    cols = []
    for e in order:
        off, wd = (e * 128, 128) if e < 8 else (1024 + (e - 8) * 256, 256)
        cols += list(range(off, off + wd))
    w1, w2 = i["L3_ffn_w1"][:, cols], i["L3_ffn_w2"][cols]
    a["l3_w1"] = np.stack([k_major(w1[:, p * FF:(p + 1) * FF]) for p in range(4)])
    a["l3_w2"] = np.stack([hidden_major(w2[p * FF:(p + 1) * FF]) for p in range(4)])
    return {n: np.ascontiguousarray(v) for n, v in a.items()}


def kernel(**inputs):
    import concourse.bacc as bacc
    from concourse.bass_utils import run_bass_kernel_spmd as run

    nc = bacc.Bacc("TRN2", target_bir_lowering=False, num_devices=1)
    arrays = {f"in_{n}": v for n, v in lay_out(inputs).items()}
    a = {n[3:]: nc.dram_tensor(n, v.shape, mybir.dt.from_np(v.dtype), kind="ExternalInput").ap()
         for n, v in arrays.items()}
    out = nc.dram_tensor("out", (BATCH, SEQ, DIM), F32, kind="ExternalOutput").ap()
    build(nc, a, out.rearrange("(t b) s d -> (b s) t d", t=NT), STOP)
    r = run(nc, [arrays], core_ids=[0])
    return r.results[0]["out"]


STOP = 99
```
